# Optimizing a Trainium2 kernel written in Bass

```python
import numpy as np
import jax
import jax.numpy as jnp

def _softmax(x, axis=-1):
    return jax.nn.softmax(x, axis=axis)

def _gelu(x):
    return jax.nn.gelu(x, approximate=True)

def _silu(x):
    return jax.nn.silu(x)

def _sigmoid(x):
    return jax.nn.sigmoid(x)

def _layernorm(x, axis=-1, eps=1e-05):
    m = jnp.mean(x, axis=axis, keepdims=True)
    v = jnp.var(x, axis=axis, keepdims=True)
    return (x - m) / jnp.sqrt(v + eps)

def _scatter_add(tgt, idx, src, axis=0):
    return tgt.at[idx].add(src)

def _segment_sum(src, seg, n):
    return jax.ops.segment_sum(src, seg, n)
kernel_name = 'mk_dlrm_tower_d1_rec_r8_887ed9'

def setup_inputs(seed: int=0):
    np.random.seed(seed)
    _w = jnp.asarray

    def _rec_inputs():
        import jax
        import jax.numpy as jnp
        _tk = jax.random.key(seed)
        ids = jnp.stack([jax.random.randint(jax.random.fold_in(_tk, 200 + f), (2048,), 0, v, jnp.int32) for f, v in enumerate([1250, 125000, 12500, 1000, 12500, 12500, 12500, 1000, 1250, 1000, 1000, 1000, 12500, 1000, 1250, 1000, 12500, 1000, 12500, 12500, 1250, 1000, 1000, 12500, 1000, 1000])], axis=1)
        tbl_0 = 0.05 * jax.random.normal(jax.random.fold_in(_tk, 500 + 0), (1250, 128), jnp.float32)
        tbl_1 = 0.05 * jax.random.normal(jax.random.fold_in(_tk, 500 + 1), (125000, 128), jnp.float32)
        tbl_2 = 0.05 * jax.random.normal(jax.random.fold_in(_tk, 500 + 2), (12500, 128), jnp.float32)
        tbl_3 = 0.05 * jax.random.normal(jax.random.fold_in(_tk, 500 + 3), (1000, 128), jnp.float32)
        tbl_4 = 0.05 * jax.random.normal(jax.random.fold_in(_tk, 500 + 4), (12500, 128), jnp.float32)
        tbl_5 = 0.05 * jax.random.normal(jax.random.fold_in(_tk, 500 + 5), (12500, 128), jnp.float32)
        tbl_6 = 0.05 * jax.random.normal(jax.random.fold_in(_tk, 500 + 6), (12500, 128), jnp.float32)
        tbl_7 = 0.05 * jax.random.normal(jax.random.fold_in(_tk, 500 + 7), (1000, 128), jnp.float32)
        tbl_8 = 0.05 * jax.random.normal(jax.random.fold_in(_tk, 500 + 8), (1250, 128), jnp.float32)
        tbl_9 = 0.05 * jax.random.normal(jax.random.fold_in(_tk, 500 + 9), (1000, 128), jnp.float32)
        tbl_10 = 0.05 * jax.random.normal(jax.random.fold_in(_tk, 500 + 10), (1000, 128), jnp.float32)
        tbl_11 = 0.05 * jax.random.normal(jax.random.fold_in(_tk, 500 + 11), (1000, 128), jnp.float32)
        tbl_12 = 0.05 * jax.random.normal(jax.random.fold_in(_tk, 500 + 12), (12500, 128), jnp.float32)
        tbl_13 = 0.05 * jax.random.normal(jax.random.fold_in(_tk, 500 + 13), (1000, 128), jnp.float32)
        tbl_14 = 0.05 * jax.random.normal(jax.random.fold_in(_tk, 500 + 14), (1250, 128), jnp.float32)
        tbl_15 = 0.05 * jax.random.normal(jax.random.fold_in(_tk, 500 + 15), (1000, 128), jnp.float32)
        tbl_16 = 0.05 * jax.random.normal(jax.random.fold_in(_tk, 500 + 16), (12500, 128), jnp.float32)
        tbl_17 = 0.05 * jax.random.normal(jax.random.fold_in(_tk, 500 + 17), (1000, 128), jnp.float32)
        tbl_18 = 0.05 * jax.random.normal(jax.random.fold_in(_tk, 500 + 18), (12500, 128), jnp.float32)
        tbl_19 = 0.05 * jax.random.normal(jax.random.fold_in(_tk, 500 + 19), (12500, 128), jnp.float32)
        tbl_20 = 0.05 * jax.random.normal(jax.random.fold_in(_tk, 500 + 20), (1250, 128), jnp.float32)
        tbl_21 = 0.05 * jax.random.normal(jax.random.fold_in(_tk, 500 + 21), (1000, 128), jnp.float32)
        tbl_22 = 0.05 * jax.random.normal(jax.random.fold_in(_tk, 500 + 22), (1000, 128), jnp.float32)
        tbl_23 = 0.05 * jax.random.normal(jax.random.fold_in(_tk, 500 + 23), (12500, 128), jnp.float32)
        tbl_24 = 0.05 * jax.random.normal(jax.random.fold_in(_tk, 500 + 24), (1000, 128), jnp.float32)
        tbl_25 = 0.05 * jax.random.normal(jax.random.fold_in(_tk, 500 + 25), (1000, 128), jnp.float32)
        _rk = jax.random.fold_in(_tk, 7)
        r_dense_features = -0.000520686 + 1.00062 * jax.random.normal(jax.random.fold_in(_rk, 101), (2048, 128), jnp.float32)
        W_top1 = 0.0405887 * jax.random.normal(jax.random.fold_in(_tk, 801), (607, 512), jnp.float32)
        W_top2 = 0.0441942 * jax.random.normal(jax.random.fold_in(_tk, 802), (512, 256), jnp.float32)
        W_top3 = 0.0625 * jax.random.normal(jax.random.fold_in(_tk, 803), (256, 1), jnp.float32)
        b_top1 = jnp.zeros((512,), jnp.float32)
        b_top2 = jnp.zeros((256,), jnp.float32)
        return (r_dense_features, ids, tbl_0, tbl_1, tbl_2, tbl_3, tbl_4, tbl_5, tbl_6, tbl_7, tbl_8, tbl_9, tbl_10, tbl_11, tbl_12, tbl_13, tbl_14, tbl_15, tbl_16, tbl_17, tbl_18, tbl_19, tbl_20, tbl_21, tbl_22, tbl_23, tbl_24, tbl_25, W_top1, b_top1, W_top2, b_top2, W_top3)
    r_dense_features, ids, tbl_0, tbl_1, tbl_2, tbl_3, tbl_4, tbl_5, tbl_6, tbl_7, tbl_8, tbl_9, tbl_10, tbl_11, tbl_12, tbl_13, tbl_14, tbl_15, tbl_16, tbl_17, tbl_18, tbl_19, tbl_20, tbl_21, tbl_22, tbl_23, tbl_24, tbl_25, W_top1, b_top1, W_top2, b_top2, W_top3 = _rec_inputs()

    def _L0_rec_setup():
        import jax, jax.numpy as jnp
        import numpy as np
        NUM_SPARSE = 26
        EMBED_DIM = 128
        BATCH = 2048
        key = jax.random.key(seed)
        k1, k2 = jax.random.split(key)
        dense_features = jax.random.normal(k1, (BATCH, EMBED_DIM), dtype=jnp.float32)
        sparse_features = jax.random.normal(k2, (BATCH, NUM_SPARSE, EMBED_DIM), dtype=jnp.float32)
        return {'dense_features': dense_features, 'sparse_features': sparse_features}
    _L0_rec_all = _L0_rec_setup()
    _L0_rec_in = {k: v for k, v in _L0_rec_all.items() if k in ()}
    del _L0_rec_all
    return {'r_dense_features': r_dense_features, 'ids': ids, 'tbl_0': tbl_0, 'tbl_1': tbl_1, 'tbl_2': tbl_2, 'tbl_3': tbl_3, 'tbl_4': tbl_4, 'tbl_5': tbl_5, 'tbl_6': tbl_6, 'tbl_7': tbl_7, 'tbl_8': tbl_8, 'tbl_9': tbl_9, 'tbl_10': tbl_10, 'tbl_11': tbl_11, 'tbl_12': tbl_12, 'tbl_13': tbl_13, 'tbl_14': tbl_14, 'tbl_15': tbl_15, 'tbl_16': tbl_16, 'tbl_17': tbl_17, 'tbl_18': tbl_18, 'tbl_19': tbl_19, 'tbl_20': tbl_20, 'tbl_21': tbl_21, 'tbl_22': tbl_22, 'tbl_23': tbl_23, 'tbl_24': tbl_24, 'tbl_25': tbl_25, 'W_top1': W_top1, 'b_top1': b_top1, 'W_top2': W_top2, 'b_top2': b_top2, 'W_top3': W_top3}

def reference(r_dense_features, ids, tbl_0, tbl_1, tbl_2, tbl_3, tbl_4, tbl_5, tbl_6, tbl_7, tbl_8, tbl_9, tbl_10, tbl_11, tbl_12, tbl_13, tbl_14, tbl_15, tbl_16, tbl_17, tbl_18, tbl_19, tbl_20, tbl_21, tbl_22, tbl_23, tbl_24, tbl_25, W_top1, b_top1, W_top2, b_top2, W_top3):
    import jax
    import jax.numpy as jnp

    def _L0_rec_ref(dense_features, sparse_features):
        import jax, jax.numpy as jnp
        import numpy as np
        NUM_SPARSE = 26
        EMBED_DIM = 128
        BATCH = 2048
        F = NUM_SPARSE + 1
        combined = jnp.concatenate([dense_features[:, None, :], sparse_features], axis=1)
        interactions = jnp.einsum('bfd,bgd->bfg', combined, combined)
        iu, ju = jnp.triu_indices(F, k=1)
        interactions_flat = interactions[:, iu, ju]
        return jnp.concatenate([dense_features, interactions_flat], axis=1)
    e = jnp.stack([tbl_0[ids[:, 0]], tbl_1[ids[:, 1]], tbl_2[ids[:, 2]], tbl_3[ids[:, 3]], tbl_4[ids[:, 4]], tbl_5[ids[:, 5]], tbl_6[ids[:, 6]], tbl_7[ids[:, 7]], tbl_8[ids[:, 8]], tbl_9[ids[:, 9]], tbl_10[ids[:, 10]], tbl_11[ids[:, 11]], tbl_12[ids[:, 12]], tbl_13[ids[:, 13]], tbl_14[ids[:, 14]], tbl_15[ids[:, 15]], tbl_16[ids[:, 16]], tbl_17[ids[:, 17]], tbl_18[ids[:, 18]], tbl_19[ids[:, 19]], tbl_20[ids[:, 20]], tbl_21[ids[:, 21]], tbl_22[ids[:, 22]], tbl_23[ids[:, 23]], tbl_24[ids[:, 24]], tbl_25[ids[:, 25]]], axis=1)
    z = _L0_rec_ref(r_dense_features, e)
    z = z.reshape(z.shape[0], -1)
    h = jnp.concatenate([z, r_dense_features], axis=1)
    h = jnp.maximum(h @ W_top1 + b_top1, 0.0)
    h = jnp.maximum(h @ W_top2 + b_top2, 0.0)
    y = h @ W_top3
    return y

_drawn_inputs = setup_inputs


def setup_inputs(seed=0):
    import zlib

    import numpy as np

    out = dict(_drawn_inputs(seed))
    spreads = {'b_top1': (0.0, 0.1), 'b_top2': (0.0, 0.1)}
    factors = {}
    for name, (base, spread) in spreads.items():
        noise = np.random.default_rng([zlib.crc32(name.encode()), seed]).standard_normal(out[name].shape)
        drawn = base * np.exp(spread * noise) if base else spread * noise
        out[name] = jnp.asarray(drawn.astype(out[name].dtype))
    for name, factor in factors.items():
        out[name] = (out[name] * factor).astype(out[name].dtype)
    return out
```

```python
from contextlib import ExitStack

import concourse.bass as bass
import numpy as np
from concourse import mybir

BATCH, FIELDS, DIM = 2048, 26, 128
FEATURES = FIELDS + 1
SMALL_ROWS = 1000
ONEHOT = [3, 7, 9, 10, 11, 13, 15, 17]
GATHER = [f for f in range(FIELDS) if f not in ONEHOT]
SLOTS = [0] + [1 + f for f in GATHER] + [1 + f for f in ONEHOT]
HALF = 128
BLOCK = 2 * HALF
BLOCKS = BATCH // BLOCK
SHIFTS = FEATURES // 2
PAIR_F = 9
PAIR_CHUNKS = FEATURES // PAIR_F
PAIR_ROWS = PAIR_F * SHIFTS
N1, N2 = 512, 256


def build_tower(nc, dense_t, gather_ids, onehot_ids, tables, small_tables, row_numbers,
                identity, w1_pairs, w1_dense, b1, w2, b2, w3, out):
    f32, f32r, i32 = mybir.dt.float32, mybir.dt.float32r, mybir.dt.int32
    ALU, ACT = mybir.AluOpType, mybir.ActivationFunctionType

    NG, NO = len(GATHER), len(ONEHOT)
    GROUP = 4
    GROUPS = [(s, min(GROUP, NG - s)) for s in range(0, NG, GROUP)]
    NGR = len(GROUPS)
    TCHUNKS = 8
    TPART = SMALL_ROWS // TCHUNKS
    PAIRS = NO // 2
    QUADS, QROWS = 4, 32
    BANK_ROWS = QROWS // 2
    WRAP = FEATURES + SHIFTS
    TB = BLOCK // QUADS
    PITCH = WRAP * TB
    XCHUNKS = PAIR_CHUNKS + 1
    K1, K2 = N1 // 128, N2 // 128

    scratch = nc.dram_tensor("interaction_scratch", (128, PITCH), f32, kind="Internal").ap()

    ctx = ExitStack()
    with ctx:
        def sb(name, shape, dt=f32):
            return ctx.enter_context(nc.sbuf_tensor(name, shape, dt))

        def sem(name):
            return ctx.enter_context(nc.semaphore(name))

        ident = sb("ident", [128, 128])
        rownum = sb("rownum", [TPART, TCHUNKS])
        idx = [sb(f"idx{h}", [128, NG], i32) for h in range(2)]
        oh_ids = sb("oh_ids", [TPART, NO, BLOCK], i32)
        rows = [sb(f"rows{h}", [128, NG, DIM]) for h in range(2)]
        EW = HALF * FEATURES
        emb = [sb(f"emb{h}", [128, EW + 32 - FEATURES]) for h in range(2)]
        stage = [sb(f"stage{s}", [128, 1024]) for s in range(2)]
        tbl = [sb(f"tbl_{p}", [TPART, NO, TCHUNKS, DIM], f32r) for p in ("hi", "lo")]
        onehot = [sb(f"onehot{s}", [TPART, TCHUNKS, BLOCK], f32r) for s in range(2)]
        dense = sb("dense", [128, BLOCK])
        inter = sb("inter", [128, WRAP, TB])
        x = sb("x", [128, XCHUNKS, BLOCK])
        xr = [sb(f"x_{p}", [128, XCHUNKS, BLOCK], f32r) for p in ("hi", "lo")]
        w1r = [sb(f"w1_{p}", [128, XCHUNKS, N1], f32r) for p in ("hi", "lo")]
        w2r = [sb(f"w2_{p}", [128, K1, N2], f32r) for p in ("hi", "lo")]
        w3s = sb("w3s", [128, K2])
        b1s = sb("b1s", [128, K1])
        b2s = sb("b2s", [128, K2])
        h1 = sb("h1", [128, K1, BLOCK])
        h1r = [sb(f"h1_{p}", [128, K1, BLOCK], f32r) for p in ("hi", "lo")]
        h2 = sb("h2", [128, K2, BLOCK])
        ycol = sb("ycol", [128, 2 * BLOCKS])
        yrow = sb("yrow", [2 * BLOCKS, 128])

        def pb(name):
            return ctx.enter_context(nc.psum_tensor(name, [128, 512], f32))

        ps_t = [pb(f"ps_t{b}") for b in range(2)]
        ps_o = [pb(f"ps_o{b}") for b in range(2)]
        ps_g = [pb(f"ps_g{b}") for b in range(2)]
        ps_m = [pb(f"ps_m{b}") for b in range(2)]

        consts_loaded = sem("consts_loaded")
        stage_loaded = [sem(f"stage_loaded{s}") for s in range(2)]
        idx_loaded = [sem(f"idx_loaded{h}") for h in range(2)]
        oh_ids_loaded = sem("oh_ids_loaded")
        dense_loaded = sem("dense_loaded")
        gathered = [[sem(f"gathered{h}_{g}") for g in range(NGR)] for h in range(2)]
        stage_split = sem("stage_split")
        onehot_ready = sem("onehot_ready")
        onehot_used = sem("onehot_used")
        onehot_placed = sem("onehot_placed")
        dense_placed = sem("dense_placed")
        transposed = sem("transposed")
        rows_placed = sem("rows_placed")
        gram_done = sem("gram_done")
        gram_copied = sem("gram_copied")
        inter_stored = sem("inter_stored")
        x_loaded = [sem(f"x_loaded{c}") for c in range(XCHUNKS)]
        staged = sem("staged")
        x_hi = sem("x_hi")
        h1_hi = sem("h1_hi")
        x_split = sem("x_split")
        l1_done = sem("l1_done")
        h1_ready = sem("h1_ready")
        h1_split = sem("h1_split")
        l2_done = sem("l2_done")
        h2_ready = sem("h2_ready")
        l3_done = sem("l3_done")
        y_copied = sem("y_copied")
        y_turned = sem("y_turned")
        y_row = sem("y_row")
        pool_step, sp_step, dve_step = sem("pool_step"), sem("sp_step"), sem("dve_step")
        out_stored = sem("out_stored")

        def wait(eng, s, value):
            if not isinstance(value, int) or value > 0:
                eng.wait_ge(s, value)

        items = [(small_tables[k].rearrange("(p c) d -> p (c d)", c=TCHUNKS), TPART, TCHUNKS * DIM)
                 for k in range(NO)]
        items += [(w1_pairs[:, 0:2, :].rearrange("p c n -> p (c n)"), PAIR_ROWS, 2 * N1),
                  (w1_pairs[:, 2, :], PAIR_ROWS, N1),
                  (w1_dense.rearrange("p c n -> p (c n)"), 128, 2 * N1),
                  (w2.rearrange("p c n -> p (c n)"), 128, K1 * N2)]

        block = ctx.enter_context(nc.Block())

        @block.sync
        def _(sp):
            def load_idx(i, h):
                sp.dma_start(idx[h][:, :], gather_ids[2 * i + h]).then_inc(idx_loaded[h], 16)

            def load_oh_ids(i):
                src = onehot_ids[i]
                sp.dma_start(oh_ids[:, :, :].rearrange("p k b -> p (k b)"),
                             src.to_broadcast([TPART, NO * BLOCK])).then_inc(oh_ids_loaded, 16)

            def load_dense(i):
                sp.dma_start(dense[:, :], dense_t[i]).then_inc(dense_loaded, 16)

            def load_stage(n):
                src, r, w = items[n]
                if n >= 2:
                    sp.wait_ge(stage_split, n - 1)
                sp.dma_start(stage[n % 2][0:r, 0:w], src).then_inc(stage_loaded[n % 2], 16)

            def next_block_loads(i):
                sp.wait_ge(transposed, 2 * NGR * i + NGR)
                sp.sem_inc(sp_step, 1)
                load_idx(i + 1, 0)
                sp.wait_ge(onehot_ready, NO * (i + 1))
                sp.sem_inc(sp_step, 1)
                load_oh_ids(i + 1)
                sp.wait_ge(dense_placed, 2 * (i + 1))
                sp.sem_inc(sp_step, 1)
                load_dense(i + 1)
                sp.wait_ge(transposed, 2 * NGR * i + 2 * NGR)
                sp.sem_inc(sp_step, 1)
                load_idx(i + 1, 1)

            def turn_interactions(i):
                sp.wait_ge(gram_copied, 8 * (i + 1))
                sp.sem_inc(sp_step, 1)
                wait(sp, x_split, XCHUNKS * i)
                sp.dma_start(scratch, inter[:, :, :].rearrange("p g t -> p (g t)")
                             ).then_inc(inter_stored, 16)
                sp.dma_start(x[:, PAIR_CHUNKS, :], dense_t[i]).then_inc(x_loaded[PAIR_CHUNKS], 16)
                sp.wait_ge(inter_stored, 16 * (i + 1))
                for c in range(PAIR_CHUNKS):
                    for j in range(QUADS):
                        src = bass.AP(tensor=scratch.tensor,
                                      offset=(QROWS * j + PAIR_F * c) * PITCH + (PAIR_F * c + 1) * TB,
                                      ap=[[PITCH + TB, PAIR_F], [TB, SHIFTS], [1, TB]])
                        sp.dma_start(x[0:PAIR_ROWS, c, TB * j:TB * (j + 1)], src
                                     ).then_inc(x_loaded[c], 16)

            load_idx(0, 0)
            load_idx(0, 1)
            sp.dma_start(rownum[:, :], row_numbers).then_inc(consts_loaded, 16)
            load_oh_ids(0)
            load_stage(0)
            load_stage(1)
            load_dense(0)
            for dst, src in ((ident, identity), (w3s, w3), (b1s, b1), (b2s, b2)):
                sp.dma_start(dst[:, :], src).then_inc(consts_loaded, 16)
            for n in range(2, len(items)):
                load_stage(n)
            next_block_loads(0)
            turn_interactions(0)
            with sp.Fori(1, BLOCKS - 1) as i:
                next_block_loads(i)
                turn_interactions(i)
            turn_interactions(BLOCKS - 1)
            sp.wait_ge(y_row, 1)
            sp.dma_start(out, yrow[:, :]).then_inc(out_stored, 16)
            sp.wait_ge(out_stored, 16)

        @block.gpsimd
        def _(pool):
            def gather_half(i, h):
                pool.wait_ge(idx_loaded[h], 16 * (i + 1))
                for g, (s, n) in enumerate(GROUPS):
                    wait(pool, transposed, 2 * NGR * (i - 1) + NGR * h + g + 1)
                    pool.sem_inc(pool_step, 1)
                    for k in range(s, s + n):
                        pool.indirect_dma_start(
                            rows[h][:, k, :], None, tables[k],
                            bass.IndirectOffsetOnAxis(ap=idx[h][:, k:k + 1], axis=0),
                        ).then_inc(gathered[h][g], 16)

            gather_half(0, 0)
            gather_half(0, 1)
            with pool.Fori(1, BLOCKS) as i:
                gather_half(i, 0)
                gather_half(i, 1)

        @block.tensor
        def _(pe):
            def onehot_lookups(i, pairs):
                for u in pairs:
                    for k in (2 * u, 2 * u + 1):
                        if isinstance(i, int):
                            pe.wait_ge(stage_split, k + 1)
                        pe.wait_ge(onehot_ready, NO * i + k + 1)
                        if k % 2 == 0:
                            wait(pe, onehot_placed, 2 * (PAIRS * i + u - 1))
                        o = ps_o[u % 2][:, BLOCK * (k % 2):BLOCK * (k % 2 + 1)]
                        for c in range(TCHUNKS):
                            for p in range(2):
                                mm = pe.matmul(o, tbl[p][:, k, c, :], onehot[k % 2][:, c, :],
                                               start=(c + p == 0), stop=(c == TCHUNKS - 1 and p == 1))
                        mm.then_inc(onehot_used, 1)

            def transposes(i, h):
                for g, (s, n) in enumerate(GROUPS):
                    q = NGR * h + g
                    pe.wait_ge(gathered[h][g], 16 * n * (i + 1))
                    wait(pe, rows_placed, 2 * NGR * i + q - 1)
                    for k in range(n):
                        mm = pe.transpose(ps_t[q % 2][:, 128 * k:128 * (k + 1)], rows[h][:, s + k, :],
                                          ident[:, :])
                    mm.then_inc(transposed, 1)

            def grams(i, h):
                pe.wait_ge(rows_placed, 2 * NGR * i + NGR * (h + 1))
                pe.wait_ge(onehot_placed, NO * (i + 1))
                pe.wait_ge(dense_placed, 2 * (i + 1))
                for q in range(2):
                    wait(pe, gram_copied, 2 * (4 * i + 2 * h + q - 1))
                    for u in range(BANK_ROWS):
                        for j in range(QUADS):
                            a = (QROWS * j + BANK_ROWS * q + u) * FEATURES
                            mm = pe.matmul(
                                ps_g[q][QROWS * j:QROWS * (j + 1), FEATURES * u:FEATURES * (u + 1)],
                                emb[h][:, a:a + QROWS], emb[h][:, a:a + FEATURES],
                                start=True, stop=True, tile_position=(0, QROWS * j))
                    mm.then_inc(gram_done, 1)

            def split_products(o, w, v, chunks, n):
                terms = [(c, a, b) for c in chunks for a, b in ((0, 0), (0, 1), (1, 0))]
                for m, (c, a, b) in enumerate(terms):
                    r = PAIR_ROWS if w is w1r and c < PAIR_CHUNKS else 128
                    mm = pe.matmul(o, w[a][0:r, c, 128 * n:128 * (n + 1)], v[b][0:r, c, :],
                                   start=(m == 0), stop=(m == len(terms) - 1))
                return mm

            def layer1(m):
                pe.wait_ge(x_split, XCHUNKS * (m + 1))
                for n in range(K1):
                    if n == 0:
                        wait(pe, h2_ready, K2 * m)
                    if n == 2:
                        wait(pe, y_copied, m)
                    o = ps_m[n // 2][:, BLOCK * (n % 2):BLOCK * (n % 2 + 1)]
                    split_products(o, w1r, xr, range(XCHUNKS), n).then_inc(l1_done, 1)

            def layer2(m):
                pe.wait_ge(h1_split, 2 * (m + 1))
                for n in range(K2):
                    o = ps_m[0][:, BLOCK * n:BLOCK * (n + 1)]
                    split_products(o, w2r, h1r, range(K1), n).then_inc(l2_done, 1)

            def layer3(m):
                pe.wait_ge(h2_ready, K2 * (m + 1))
                for t in range(2):
                    for c in range(K2):
                        mm = pe.matmul(ps_m[1][:, t:t + 1], h2[:, c, 128 * t:128 * (t + 1)],
                                       w3s[:, c:c + 1], start=(c == 0), stop=(c == K2 - 1))
                mm.then_inc(l3_done, 1)

            def front(i, between):
                onehot_lookups(i, range(PAIRS - 1))
                transposes(i, 0)
                onehot_lookups(i, [PAIRS - 1])
                grams(i, 0)
                if between:
                    layer1(i - 1)
                transposes(i, 1)
                if between:
                    layer2(i - 1)
                grams(i, 1)
                if between:
                    layer3(i - 1)

            pe.wait_ge(consts_loaded, 16 * 5)
            front(0, False)
            pe.wait_ge(stage_split, len(items))
            with pe.Fori(1, BLOCKS) as i:
                front(i, True)
            layer1(BLOCKS - 1)
            layer2(BLOCKS - 1)
            layer3(BLOCKS - 1)
            pe.wait_ge(y_copied, BLOCKS)
            pe.transpose(ps_t[0][0:2 * BLOCKS, 0:128], ycol[:, :], ident[:, :]).then_inc(y_turned, 1)

        @block.scalar
        def _(act):
            def emb_view(h):
                return emb[h][:, 0:EW].rearrange("d (r f) -> d r f", f=FEATURES)

            def place_onehot(i, pairs):
                for u in pairs:
                    if u == 0:
                        wait(act, gram_done, 4 * i)
                    act.wait_ge(onehot_used, NO * i + 2 * u + 2)
                    f = 1 + NG + 2 * u
                    for h in range(2):
                        for k in range(2):
                            src = ps_o[u % 2][:, BLOCK * k:BLOCK * (k + 1)].rearrange(
                                "d (j h t) -> d j h t", h=2, t=QROWS)[:, :, h, :]
                            dst = emb_view(h)[:, :, f + k].rearrange("d (j t) -> d j t", t=QROWS)
                            op = nc.scalar.activation(dst, src, ACT.Copy)
                        op.then_inc(onehot_placed, 1)

            def place_rows(i, h):
                wait(act, gram_done, 4 * (i - 1) + 2 * (h + 1))
                for g, (s, n) in enumerate(GROUPS):
                    q = NGR * h + g
                    act.wait_ge(transposed, 2 * NGR * i + q + 1)
                    src = ps_t[q % 2][:, 0:128 * n].rearrange("d (k r) -> d r k", r=128)
                    nc.scalar.activation(emb_view(h)[:, :, 1 + s:1 + s + n], src, ACT.Copy
                                         ).then_inc(rows_placed, 1)

            def copy_grams(i, h):
                if h == 0:
                    wait(act, inter_stored, 16 * i)
                for q in range(2):
                    act.wait_ge(gram_done, 4 * i + 2 * h + q + 1)
                    src = ps_g[q][:, 0:BANK_ROWS * FEATURES].rearrange("p (t g) -> p g t", g=FEATURES)
                    t = QROWS * h + BANK_ROWS * q
                    nc.scalar.activation(inter[:, 0:FEATURES, t:t + BANK_ROWS], src, ACT.Copy
                                         ).then_inc(gram_copied, 1)
                    nc.scalar.activation(inter[:, FEATURES:WRAP, t:t + BANK_ROWS], src[:, 0:SHIFTS, :],
                                         ACT.Copy).then_inc(gram_copied, 1)

            def relu1(m):
                wait(act, h1_split, 2 * m)
                for n in range(K1):
                    if n % 2 == 0:
                        act.wait_ge(l1_done, K1 * m + n + 2)
                    nc.scalar.activation(h1[:, n, :], ps_m[n // 2][:, BLOCK * (n % 2):BLOCK * (n % 2 + 1)],
                                         ACT.Relu, bias=b1s[:, n:n + 1]).then_inc(h1_ready, 1)

            def relu2(m):
                wait(act, l3_done, m)
                act.wait_ge(l2_done, K2 * (m + 1))
                for n in range(K2):
                    nc.scalar.activation(h2[:, n, :], ps_m[0][:, BLOCK * n:BLOCK * (n + 1)],
                                         ACT.Relu, bias=b2s[:, n:n + 1]).then_inc(h2_ready, 1)

            def body(i, between):
                place_onehot(i, range(PAIRS - 1))
                place_rows(i, 0)
                place_onehot(i, [PAIRS - 1])
                copy_grams(i, 0)
                if between:
                    relu1(i - 1)
                place_rows(i, 1)
                if between:
                    relu2(i - 1)
                copy_grams(i, 1)

            act.wait_ge(consts_loaded, 16 * 5)
            body(0, False)
            with act.Fori(1, BLOCKS) as i:
                body(i, True)
            relu1(BLOCKS - 1)
            relu2(BLOCKS - 1)

        @block.vector
        def _(dve):
            count = [0]

            def in_order(op):
                op.then_inc(staged, 1)
                count[0] += 1
                dve.wait_ge(staged, count[0])

            def split_stage(n):
                src, r, w = items[n]
                dve.wait_ge(stage_loaded[n % 2], 16 * (n // 2 + 1))
                s = stage[n % 2]
                if n < NO:
                    parts = [t[:, n, :, :].rearrange("p c d -> p (c d)") for t in tbl]
                elif n == NO:
                    parts = [t[0:r, 0:2, :].rearrange("p c n -> p (c n)") for t in w1r]
                elif n == NO + 1:
                    parts = [t[0:r, 2, :] for t in w1r]
                elif n == NO + 2:
                    in_order(nc.vector.tensor_tensor(s[:, 0:N1], s[:, 0:N1], s[:, N1:2 * N1], ALU.add))
                    parts, w = [t[:, PAIR_CHUNKS, :] for t in w1r], N1
                else:
                    parts = [t[:, :, :].rearrange("p c n -> p (c n)") for t in w2r]
                hi, lo = parts
                in_order(nc.vector.tensor_copy(hi, s[0:r, 0:w]))
                nc.vector.tensor_tensor(lo, s[0:r, 0:w], hi.bitcast(f32), ALU.subtract
                                        ).then_inc(stage_split, 1)

            def make_onehot(i, k):
                if k == 0:
                    dve.wait_ge(oh_ids_loaded, 16 * (i + 1))
                wait(dve, onehot_used, NO * i + k - 1)
                for c in range(TCHUNKS):
                    op = nc.vector.tensor_scalar(onehot[k % 2][:, c, :], oh_ids[:, k, :],
                                                 rownum[:, c:c + 1], None, ALU.is_equal)
                op.then_inc(onehot_ready, 1)

            def place_dense(i):
                dve.wait_ge(dense_loaded, 16 * (i + 1))
                wait(dve, gram_done, 4 * i)
                for h in range(2):
                    src = dense[:, :].rearrange("d (j h t) -> d j h t", h=2, t=QROWS)[:, :, h, :]
                    dst = emb[h][:, 0:EW].rearrange("d (j t f) -> d j t f", t=QROWS, f=FEATURES)
                    nc.vector.tensor_copy(dst[:, :, :, 0], src).then_inc(dense_placed, 1)

            def split_x(m):
                wait(dve, l1_done, K1 * m)
                for c in (PAIR_CHUNKS, *range(PAIR_CHUNKS)):
                    r, n = (128, 1) if c == PAIR_CHUNKS else (PAIR_ROWS, QUADS)
                    dve.wait_ge(x_loaded[c], 16 * n * (m + 1))
                    nc.vector.tensor_copy(xr[0][0:r, c, :], x[0:r, c, :]).then_inc(x_hi, 1)
                    dve.wait_ge(x_hi, XCHUNKS * m + (c + 1) % XCHUNKS + 1)
                    nc.vector.tensor_tensor(xr[1][0:r, c, :], x[0:r, c, :],
                                            xr[0][0:r, c, :].bitcast(f32), ALU.subtract
                                            ).then_inc(x_split, 1)

            def split_h1(m):
                wait(dve, l2_done, K2 * m)
                for a in range(2):
                    dve.wait_ge(h1_ready, K1 * m + 2 * a + 2)
                    part = [t[:, 2 * a:2 * a + 2, :].rearrange("p c b -> p (c b)") for t in (h1, *h1r)]
                    nc.vector.tensor_copy(part[1], part[0]).then_inc(h1_hi, 1)
                    dve.wait_ge(h1_hi, 2 * m + a + 1)
                    nc.vector.tensor_tensor(part[2], part[0], part[1].bitcast(f32), ALU.subtract
                                            ).then_inc(h1_split, 1)

            def copy_y(m):
                dve.wait_ge(l3_done, m + 1)
                dve.sem_inc(dve_step, 1)
                nc.vector.tensor_copy(ycol[:, bass.ds(2 * m, 2)], ps_m[1][:, 0:2]
                                      ).then_inc(y_copied, 1)

            dve.wait_ge(consts_loaded, 16 * 5)
            for h in range(2):
                nc.vector.memset(emb[h][:, EW:], 0.0)
            for k in range(NO):
                split_stage(k)
                make_onehot(0, k)
            for n in range(NO, len(items)):
                split_stage(n)
            place_dense(0)
            for k in range(2):
                make_onehot(1, k)
            with dve.Fori(1, BLOCKS - 1) as i:
                for k in range(2, NO):
                    make_onehot(i, k)
                place_dense(i)
                split_x(i - 1)
                split_h1(i - 1)
                for k in range(2):
                    make_onehot(i + 1, k)
                copy_y(i - 1)
            last = BLOCKS - 1
            for k in range(2, NO):
                make_onehot(last, k)
            place_dense(last)
            for m in (last - 1, last):
                split_x(m)
                split_h1(m)
                copy_y(m)
            dve.wait_ge(y_turned, 1)
            nc.vector.tensor_copy(yrow[:, :], ps_t[0][0:2 * BLOCKS, 0:128]).then_inc(y_row, 1)


def kernel(**inputs):
    import concourse.bacc as bacc
    from concourse.bass_utils import run_bass_kernel_spmd

    a = {k: np.asarray(v) for k, v in inputs.items()}
    ids = a["ids"].reshape(BLOCKS, 4, 2, 32, FIELDS)
    gather_ids = ids[..., GATHER].transpose(0, 2, 1, 3, 4).reshape(2 * BLOCKS, HALF, len(GATHER))
    onehot_ids = a["ids"].reshape(BLOCKS, BLOCK, FIELDS)[..., ONEHOT].transpose(0, 2, 1)
    dense_t = a["r_dense_features"].reshape(BLOCKS, BLOCK, DIM).transpose(0, 2, 1)
    w1 = a["W_top1"]
    row_of, n = {}, DIM
    for f in range(FEATURES):
        for g in range(f + 1, FEATURES):
            row_of[f, g] = n
            n += 1
    order = [row_of[tuple(sorted((SLOTS[f], SLOTS[(f + k) % FEATURES])))]
             for f in range(FEATURES) for k in range(1, SHIFTS + 1)]
    w1_pairs = w1[order].reshape(PAIR_CHUNKS, PAIR_ROWS, N1).transpose(1, 0, 2)
    w1_dense = np.stack([w1[:DIM], w1[n:]], axis=1)
    named = {
        "dense_t": dense_t,
        "gather_ids": gather_ids,
        "onehot_ids": onehot_ids.reshape(BLOCKS, 1, len(ONEHOT) * BLOCK),
        "tables": [a[f"tbl_{f}"] for f in GATHER],
        "small_tables": [a[f"tbl_{f}"] for f in ONEHOT],
        "row_numbers": np.arange(SMALL_ROWS, dtype=np.float32).reshape(SMALL_ROWS // 8, 8),
        "identity": np.eye(128, dtype=np.float32),
        "w1_pairs": w1_pairs,
        "w1_dense": w1_dense,
        "b1": a["b_top1"].reshape(N1 // 128, 128).T,
        "w2": a["W_top2"].reshape(N1 // 128, 128, N2).transpose(1, 0, 2),
        "b2": a["b_top2"].reshape(N2 // 128, 128).T,
        "w3": a["W_top3"].reshape(N2 // 128, 128).T,
    }
    nc = bacc.Bacc("TRN2", target_bir_lowering=False, num_devices=1)
    arrays = {}

    def declare(name, array):
        array = np.ascontiguousarray(array)
        arrays[name] = array
        return nc.dram_tensor(name, array.shape, mybir.dt.from_np(array.dtype), kind="ExternalInput").ap()

    args = {}
    for name, v in named.items():
        args[name] = ([declare(f"{name}_{n}", t) for n, t in enumerate(v)] if isinstance(v, list)
                      else declare(name, v))
    args["out"] = nc.dram_tensor("out", (2 * BLOCKS, HALF), mybir.dt.float32, kind="ExternalOutput").ap()
    build_tower(nc, **args)
    result = run_bass_kernel_spmd(nc, [arrays], core_ids=[0])
    return result.results[0]["out"].reshape(BATCH, 1)
```

```python
from contextlib import ExitStack

import concourse.bass as bass
import numpy as np
from concourse import mybir

BATCH, FIELDS, DIM = 2048, 26, 128
FEATURES = FIELDS + 1
SMALL_ROWS = 1000
ONEHOT = [3, 7, 9, 10, 11, 13, 15, 17]
GATHER = [f for f in range(FIELDS) if f not in ONEHOT]
SLOTS = [0] + [1 + f for f in GATHER] + [1 + f for f in ONEHOT]
HALF = 128
BLOCK = 2 * HALF
BLOCKS = BATCH // BLOCK
SHIFTS = FEATURES // 2
PAIR_F = 9
PAIR_CHUNKS = FEATURES // PAIR_F
PAIR_ROWS = PAIR_F * SHIFTS
N1, N2 = 512, 256


def build_tower(nc, dense_t, gather_ids, onehot_ids, tables, small_tables, row_numbers,
                identity, w1_pairs, w1_dense, b1, w2, b2, w3, out):
    f32, f32r, i32 = mybir.dt.float32, mybir.dt.float32r, mybir.dt.int32
    ALU, ACT = mybir.AluOpType, mybir.ActivationFunctionType

    NG, NO = len(GATHER), len(ONEHOT)
    GROUP = 4
    GROUPS = [(s, min(GROUP, NG - s)) for s in range(0, NG, GROUP)]
    NGR = len(GROUPS)
    TCHUNKS = 8
    TPART = SMALL_ROWS // TCHUNKS
    PAIRS = NO // 2
    QUADS, QROWS = 4, 32
    BANK_ROWS = QROWS // 2
    WRAP = FEATURES + SHIFTS
    TB = BLOCK // QUADS
    PITCH = WRAP * TB
    XCHUNKS = PAIR_CHUNKS + 1
    K1, K2 = N1 // 128, N2 // 128

    scratch = nc.dram_tensor("interaction_scratch", (128, PITCH), f32, kind="Internal").ap()

    ctx = ExitStack()
    with ctx:
        def sb(name, shape, dt=f32):
            return ctx.enter_context(nc.sbuf_tensor(name, shape, dt))

        def sem(name):
            return ctx.enter_context(nc.semaphore(name))

        ident = sb("ident", [128, 128])
        rownum = sb("rownum", [TPART, TCHUNKS])
        idx = [sb(f"idx{h}", [128, NG], i32) for h in range(2)]
        oh_ids = sb("oh_ids", [TPART, NO, BLOCK], i32)
        rows = [sb(f"rows{h}", [128, NG, DIM]) for h in range(2)]
        EW = HALF * FEATURES
        emb = [sb(f"emb{h}", [128, EW + 32 - FEATURES]) for h in range(2)]
        stage = [sb(f"stage{s}", [128, 1024]) for s in range(2)]
        tbl = [sb(f"tbl_{p}", [TPART, NO, TCHUNKS, DIM], f32r) for p in ("hi", "lo")]
        onehot = [sb(f"onehot{s}", [TPART, TCHUNKS, BLOCK], f32r) for s in range(2)]
        dense = sb("dense", [128, BLOCK])
        inter = sb("inter", [128, WRAP, TB])
        x = sb("x", [128, XCHUNKS, BLOCK])
        xr = [sb(f"x_{p}", [128, XCHUNKS, BLOCK], f32r) for p in ("hi", "lo")]
        w1r = [sb(f"w1_{p}", [128, XCHUNKS, N1], f32r) for p in ("hi", "lo")]
        w2r = [sb(f"w2_{p}", [128, K1, N2], f32r) for p in ("hi", "lo")]
        w3s = sb("w3s", [128, K2])
        b1s = sb("b1s", [128, K1])
        b2s = sb("b2s", [128, K2])
        h1 = sb("h1", [128, K1, BLOCK])
        h1r = [sb(f"h1_{p}", [128, K1, BLOCK], f32r) for p in ("hi", "lo")]
        h2 = sb("h2", [128, K2, BLOCK])
        ycol = sb("ycol", [128, 2 * BLOCKS])
        yrow = sb("yrow", [2 * BLOCKS, 128])

        def pb(name):
            return ctx.enter_context(nc.psum_tensor(name, [128, 512], f32))

        ps_t = [pb(f"ps_t{b}") for b in range(2)]
        ps_o = [pb(f"ps_o{b}") for b in range(2)]
        ps_g = [pb(f"ps_g{b}") for b in range(2)]
        ps_m = [pb(f"ps_m{b}") for b in range(2)]

        consts_loaded = sem("consts_loaded")
        stage_loaded = [sem(f"stage_loaded{s}") for s in range(2)]
        idx_loaded = [sem(f"idx_loaded{h}") for h in range(2)]
        oh_ids_loaded = sem("oh_ids_loaded")
        dense_loaded = sem("dense_loaded")
        gathered = [[sem(f"gathered{h}_{g}") for g in range(NGR)] for h in range(2)]
        stage_split = sem("stage_split")
        onehot_ready = sem("onehot_ready")
        onehot_used = sem("onehot_used")
        onehot_placed = sem("onehot_placed")
        dense_placed = sem("dense_placed")
        transposed = sem("transposed")
        rows_placed = sem("rows_placed")
        gram_done = sem("gram_done")
        gram_copied = sem("gram_copied")
        inter_stored = sem("inter_stored")
        x_loaded = [sem(f"x_loaded{c}") for c in range(XCHUNKS)]
        stage_hi = sem("stage_hi")
        w1_dense_added = sem("w1_dense_added")
        x_hi = sem("x_hi")
        h1_hi = sem("h1_hi")
        x_split = sem("x_split")
        l1_done = sem("l1_done")
        h1_ready = sem("h1_ready")
        h1_split = sem("h1_split")
        l2_done = sem("l2_done")
        h2_ready = sem("h2_ready")
        l3_done = sem("l3_done")
        y_copied = sem("y_copied")
        y_turned = sem("y_turned")
        y_row = sem("y_row")
        pool_step, sp_step, dve_step = sem("pool_step"), sem("sp_step"), sem("dve_step")
        out_stored = sem("out_stored")

        def wait(eng, s, value):
            if not isinstance(value, int) or value > 0:
                eng.wait_ge(s, value)

        items = [(small_tables[k].rearrange("(p c) d -> p (c d)", c=TCHUNKS), TPART, TCHUNKS * DIM)
                 for k in range(NO)]
        items += [(w1_pairs[:, 0:2, :].rearrange("p c n -> p (c n)"), PAIR_ROWS, 2 * N1),
                  (w1_pairs[:, 2, :], PAIR_ROWS, N1),
                  (w1_dense.rearrange("p c n -> p (c n)"), 128, 2 * N1),
                  (w2.rearrange("p c n -> p (c n)"), 128, K1 * N2)]

        DENSE_ITEM = NO + 2

        def split_of(n):
            if n < NO:
                parts = [t[:, n, :, :].rearrange("p c d -> p (c d)") for t in tbl]
            elif n == NO:
                parts = [t[0:PAIR_ROWS, 0:2, :].rearrange("p c n -> p (c n)") for t in w1r]
            elif n == NO + 1:
                parts = [t[0:PAIR_ROWS, 2, :] for t in w1r]
            elif n == DENSE_ITEM:
                parts = [t[:, PAIR_CHUNKS, :] for t in w1r]
            else:
                parts = [t[:, :, :].rearrange("p c n -> p (c n)") for t in w2r]
            return (N1 if n in (NO + 1, DENSE_ITEM) else 1024, *parts)

        block = ctx.enter_context(nc.Block())

        @block.sync
        def _(sp):
            def load_idx(i, h):
                sp.dma_start(idx[h][:, :], gather_ids[2 * i + h]).then_inc(idx_loaded[h], 16)

            def load_oh_ids(i):
                src = onehot_ids[i]
                sp.dma_start(oh_ids[:, :, :].rearrange("p k b -> p (k b)"),
                             src.to_broadcast([TPART, NO * BLOCK])).then_inc(oh_ids_loaded, 16)

            def load_dense(i):
                sp.dma_start(dense[:, :], dense_t[i]).then_inc(dense_loaded, 16)

            def load_stage(n):
                src, r, w = items[n]
                if n >= 2:
                    sp.wait_ge(stage_split, n - 1)
                sp.dma_start(stage[n % 2][0:r, 0:w], src).then_inc(stage_loaded[n % 2], 16)

            def next_block_loads(i):
                sp.wait_ge(transposed, 2 * NGR * i + NGR)
                sp.sem_inc(sp_step, 1)
                load_idx(i + 1, 0)
                sp.wait_ge(onehot_ready, NO * (i + 1))
                sp.sem_inc(sp_step, 1)
                load_oh_ids(i + 1)
                sp.wait_ge(dense_placed, 2 * (i + 1))
                sp.sem_inc(sp_step, 1)
                load_dense(i + 1)
                sp.wait_ge(transposed, 2 * NGR * i + 2 * NGR)
                sp.sem_inc(sp_step, 1)
                load_idx(i + 1, 1)

            def turn_interactions(i):
                sp.wait_ge(gram_copied, 8 * (i + 1))
                sp.sem_inc(sp_step, 1)
                wait(sp, x_split, XCHUNKS * i)
                sp.dma_start(scratch, inter[:, :, :].rearrange("p g t -> p (g t)")
                             ).then_inc(inter_stored, 16)
                sp.dma_start(x[:, PAIR_CHUNKS, :], dense_t[i]).then_inc(x_loaded[PAIR_CHUNKS], 16)
                sp.wait_ge(inter_stored, 16 * (i + 1))
                for c in range(PAIR_CHUNKS):
                    for j in range(QUADS):
                        src = bass.AP(tensor=scratch.tensor,
                                      offset=(QROWS * j + PAIR_F * c) * PITCH + (PAIR_F * c + 1) * TB,
                                      ap=[[PITCH + TB, PAIR_F], [TB, SHIFTS], [1, TB]])
                        sp.dma_start(x[0:PAIR_ROWS, c, TB * j:TB * (j + 1)], src
                                     ).then_inc(x_loaded[c], 16)

            load_idx(0, 0)
            load_idx(0, 1)
            sp.dma_start(rownum[:, :], row_numbers).then_inc(consts_loaded, 16)
            load_oh_ids(0)
            load_stage(0)
            load_stage(1)
            load_dense(0)
            for dst, src in ((ident, identity), (w3s, w3), (b1s, b1), (b2s, b2)):
                sp.dma_start(dst[:, :], src).then_inc(consts_loaded, 16)
            for n in range(2, len(items)):
                load_stage(n)
            next_block_loads(0)
            turn_interactions(0)
            with sp.Fori(1, BLOCKS - 1) as i:
                next_block_loads(i)
                turn_interactions(i)
            turn_interactions(BLOCKS - 1)
            sp.wait_ge(y_row, 1)
            sp.dma_start(out, yrow[:, :]).then_inc(out_stored, 16)
            sp.wait_ge(out_stored, 16)

        @block.gpsimd
        def _(pool):
            def gather_half(i, h):
                pool.wait_ge(idx_loaded[h], 16 * (i + 1))
                for g, (s, n) in enumerate(GROUPS):
                    wait(pool, transposed, 2 * NGR * (i - 1) + NGR * h + g + 1)
                    pool.sem_inc(pool_step, 1)
                    for k in range(s, s + n):
                        pool.indirect_dma_start(
                            rows[h][:, k, :], None, tables[k],
                            bass.IndirectOffsetOnAxis(ap=idx[h][:, k:k + 1], axis=0),
                        ).then_inc(gathered[h][g], 16)

            gather_half(0, 0)
            gather_half(0, 1)
            with pool.Fori(1, BLOCKS) as i:
                gather_half(i, 0)
                gather_half(i, 1)

        @block.tensor
        def _(pe):
            def onehot_lookups(i, u):
                for k in (2 * u, 2 * u + 1):
                    if isinstance(i, int):
                        pe.wait_ge(stage_split, k + 1)
                    pe.wait_ge(onehot_ready, NO * i + k + 1)
                    if k % 2 == 0:
                        wait(pe, onehot_placed, 2 * (PAIRS * i + u - 1))
                    o = ps_o[u % 2][:, BLOCK * (k % 2):BLOCK * (k % 2 + 1)]
                    for c in range(TCHUNKS):
                        for p in range(2):
                            mm = pe.matmul(o, tbl[p][:, k, c, :], onehot[k % 2][:, c, :],
                                           start=(c + p == 0), stop=(c == TCHUNKS - 1 and p == 1))
                    mm.then_inc(onehot_used, 1)

            def transposes(i, h, g):
                s, n = GROUPS[g]
                q = NGR * h + g
                pe.wait_ge(gathered[h][g], 16 * n * (i + 1))
                wait(pe, rows_placed, 2 * NGR * i + q - 1)
                for k in range(n):
                    mm = pe.transpose(ps_t[q % 2][:, 128 * k:128 * (k + 1)], rows[h][:, s + k, :],
                                      ident[:, :])
                mm.then_inc(transposed, 1)

            def grams(i, h, q):
                if q == 0:
                    pe.wait_ge(rows_placed, 2 * NGR * i + NGR * (h + 1))
                    pe.wait_ge(onehot_placed, NO * (i + 1))
                    pe.wait_ge(dense_placed, 2 * (i + 1))
                wait(pe, gram_copied, 2 * (4 * i + 2 * h + q - 1))
                for u in range(BANK_ROWS):
                    for j in range(QUADS):
                        a = (QROWS * j + BANK_ROWS * q + u) * FEATURES
                        mm = pe.matmul(
                            ps_g[q][QROWS * j:QROWS * (j + 1), FEATURES * u:FEATURES * (u + 1)],
                            emb[h][:, a:a + QROWS], emb[h][:, a:a + FEATURES],
                            start=True, stop=True, tile_position=(0, QROWS * j))
                mm.then_inc(gram_done, 1)

            def split_products(o, w, v, chunks, n, ready=None):
                terms = [(c, a, b) for c in chunks for a, b in ((0, 0), (0, 1), (1, 0))]
                for m, (c, a, b) in enumerate(terms):
                    if ready and (a, b) == (0, 0):
                        pe.wait_ge(*ready(c))
                    r = PAIR_ROWS if w is w1r and c < PAIR_CHUNKS else 128
                    mm = pe.matmul(o, w[a][0:r, c, 128 * n:128 * (n + 1)], v[b][0:r, c, :],
                                   start=(m == 0), stop=(m == len(terms) - 1))
                return mm

            def layer1(m, n):
                if n == 0:
                    wait(pe, h2_ready, K2 * m)
                if n == 2:
                    wait(pe, y_copied, m)
                o = ps_m[n // 2][:, BLOCK * (n % 2):BLOCK * (n % 2 + 1)]
                order = (PAIR_CHUNKS, *range(PAIR_CHUNKS))
                split_products(o, w1r, xr, order, n,
                               (lambda c: (x_split, XCHUNKS * m + order.index(c) + 1)) if n == 0 else None
                               ).then_inc(l1_done, 1)

            def layer2(m, n):
                if n == 0:
                    pe.wait_ge(h1_split, K1 * (m + 1))
                o = ps_m[0][:, BLOCK * n:BLOCK * (n + 1)]
                split_products(o, w2r, h1r, range(K1), n).then_inc(l2_done, 1)

            def layer3(m):
                pe.wait_ge(h2_ready, K2 * (m + 1))
                for t in range(2):
                    for c in range(K2):
                        mm = pe.matmul(ps_m[1][:, t:t + 1], h2[:, c, 128 * t:128 * (t + 1)],
                                       w3s[:, c:c + 1], start=(c == 0), stop=(c == K2 - 1))
                mm.then_inc(l3_done, 1)

            def body(i, first=False, last=False):
                for u in range(PAIRS):
                    transposes(i, 0, u)
                    onehot_lookups(i, u)
                for g in range(PAIRS, NGR):
                    transposes(i, 0, g)
                if first:
                    grams(i, 0, 0)
                    transposes(i, 1, 0)
                    transposes(i, 1, 1)
                    grams(i, 0, 1)
                    for g in range(2, NGR):
                        transposes(i, 1, g)
                    grams(i, 1, 0)
                    grams(i, 1, 1)
                    return
                layer1(i - 1, 0)
                grams(i, 0, 0)
                layer1(i - 1, 1)
                transposes(i, 1, 0)
                layer1(i - 1, 2)
                if last:
                    grams(i, 0, 1)
                    layer1(i - 1, 3)
                    transposes(i, 1, 1)
                    transposes(i, 1, 2)
                    layer2(i - 1, 0)
                    layer2(i - 1, 1)
                    transposes(i, 1, 3)
                    layer3(i - 1)
                    for g in range(4, NGR):
                        transposes(i, 1, g)
                    grams(i, 1, 0)
                    grams(i, 1, 1)
                    return
                layer1(i - 1, 3)
                transposes(i, 1, 1)
                transposes(i, 1, 2)
                grams(i, 0, 1)
                for g in range(3, NGR):
                    transposes(i, 1, g)
                layer2(i - 1, 0)
                grams(i, 1, 0)
                layer2(i - 1, 1)
                grams(i, 1, 1)
                layer3(i - 1)

            pe.wait_ge(consts_loaded, 16 * 5)
            body(0, first=True)
            pe.wait_ge(stage_split, len(items))
            with pe.Fori(1, BLOCKS - 1) as i:
                body(i)
            body(BLOCKS - 1, last=True)
            for n in range(K1):
                layer1(BLOCKS - 1, n)
            for n in range(K2):
                layer2(BLOCKS - 1, n)
            layer3(BLOCKS - 1)
            pe.wait_ge(y_copied, BLOCKS)
            pe.transpose(ps_t[0][0:2 * BLOCKS, 0:128], ycol[:, :], ident[:, :]).then_inc(y_turned, 1)

        @block.scalar
        def _(act):
            def split_hi(n):
                w, hi, lo = split_of(n)
                if n == DENSE_ITEM:
                    act.wait_ge(w1_dense_added, 1)
                act.wait_ge(stage_loaded[n % 2], 16 * (n // 2 + 1))
                nc.scalar.activation(hi, stage[n % 2][0:items[n][1], 0:w], ACT.Copy
                                     ).then_inc(stage_hi, 1)

            def emb_view(h):
                return emb[h][:, 0:EW].rearrange("d (r f) -> d r f", f=FEATURES)

            def place_onehot(i, u):
                if u == 0:
                    wait(act, gram_done, 4 * i)
                act.wait_ge(onehot_used, NO * i + 2 * u + 2)
                f = 1 + NG + 2 * u
                for h in range(2):
                    src = ps_o[u % 2][:, :].rearrange("d (k j h t) -> d k j h t", k=2, h=2, t=QROWS
                                                      )[:, :, :, h, :]
                    dst = emb_view(h)[:, :, f:f + 2].rearrange("d (j t) k -> d k j t", t=QROWS)
                    nc.scalar.activation(dst, src, ACT.Copy).then_inc(onehot_placed, 1)

            def place_rows(i, h, g):
                if g == 0:
                    wait(act, gram_done, 4 * (i - 1) + 2 * (h + 1))
                s, n = GROUPS[g]
                q = NGR * h + g
                act.wait_ge(transposed, 2 * NGR * i + q + 1)
                src = ps_t[q % 2][:, 0:128 * n].rearrange("d (k r) -> d r k", r=128)
                nc.scalar.activation(emb_view(h)[:, :, 1 + s:1 + s + n], src, ACT.Copy
                                     ).then_inc(rows_placed, 1)

            def copy_grams(i, h, q):
                if h == 0 and q == 0:
                    wait(act, inter_stored, 16 * i)
                act.wait_ge(gram_done, 4 * i + 2 * h + q + 1)
                src = ps_g[q][:, 0:BANK_ROWS * FEATURES].rearrange("p (t g) -> p g t", g=FEATURES)
                t = QROWS * h + BANK_ROWS * q
                nc.scalar.activation(inter[:, 0:FEATURES, t:t + BANK_ROWS], src, ACT.Copy
                                     ).then_inc(gram_copied, 1)
                nc.scalar.activation(inter[:, FEATURES:WRAP, t:t + BANK_ROWS], src[:, 0:SHIFTS, :],
                                     ACT.Copy).then_inc(gram_copied, 1)

            def relu1(m, bank):
                if bank == 0:
                    wait(act, h1_split, K1 * m)
                act.wait_ge(l1_done, K1 * m + 2 * bank + 2)
                for n in (2 * bank, 2 * bank + 1):
                    nc.scalar.activation(h1[:, n, :], ps_m[bank][:, BLOCK * (n % 2):BLOCK * (n % 2 + 1)],
                                         ACT.Relu, bias=b1s[:, n:n + 1]).then_inc(h1_ready, 1)

            def relu2(m):
                wait(act, l3_done, m)
                act.wait_ge(l2_done, K2 * (m + 1))
                for n in range(K2):
                    nc.scalar.activation(h2[:, n, :], ps_m[0][:, BLOCK * n:BLOCK * (n + 1)],
                                         ACT.Relu, bias=b2s[:, n:n + 1]).then_inc(h2_ready, 1)

            def body(i, first=False, last=False):
                if first:
                    split_hi(0)
                    split_hi(1)
                for u in range(PAIRS):
                    place_rows(i, 0, u)
                    if first and u + 1 < PAIRS:
                        split_hi(2 * u + 2)
                        split_hi(2 * u + 3)
                    place_onehot(i, u)
                for g in range(PAIRS, NGR):
                    place_rows(i, 0, g)
                if first:
                    for n in range(NO, len(items)):
                        split_hi(n)
                copy_grams(i, 0, 0)
                if not first:
                    relu1(i - 1, 0)
                place_rows(i, 1, 0)
                if first:
                    place_rows(i, 1, 1)
                    copy_grams(i, 0, 1)
                    place_rows(i, 1, 2)
                elif last:
                    copy_grams(i, 0, 1)
                    relu1(i - 1, 1)
                    place_rows(i, 1, 1)
                    place_rows(i, 1, 2)
                    relu2(i - 1)
                else:
                    relu1(i - 1, 1)
                    place_rows(i, 1, 1)
                    place_rows(i, 1, 2)
                    copy_grams(i, 0, 1)
                for g in range(3, NGR):
                    place_rows(i, 1, g)
                copy_grams(i, 1, 0)
                if not first and not last:
                    relu2(i - 1)
                copy_grams(i, 1, 1)

            act.wait_ge(consts_loaded, 16 * 5)
            body(0, first=True)
            with act.Fori(1, BLOCKS - 1) as i:
                body(i)
            body(BLOCKS - 1, last=True)
            relu1(BLOCKS - 1, 0)
            relu1(BLOCKS - 1, 1)
            relu2(BLOCKS - 1)

        @block.vector
        def _(dve):
            def split_lo(n):
                r = items[n][1]
                w, hi, lo = split_of(n)
                s = stage[n % 2]
                if n == DENSE_ITEM:
                    dve.wait_ge(stage_loaded[n % 2], 16 * (n // 2 + 1))
                    nc.vector.tensor_tensor(s[:, 0:N1], s[:, 0:N1], s[:, N1:2 * N1], ALU.add
                                            ).then_inc(w1_dense_added, 1)
                dve.wait_ge(stage_hi, n + 1)
                nc.vector.tensor_tensor(lo, s[0:r, 0:w], hi.bitcast(f32), ALU.subtract
                                        ).then_inc(stage_split, 1)

            def make_onehot(i, k):
                if k == 0:
                    dve.wait_ge(oh_ids_loaded, 16 * (i + 1))
                wait(dve, onehot_used, NO * i + k - 1)
                for c in range(TCHUNKS):
                    op = nc.vector.tensor_scalar(onehot[k % 2][:, c, :], oh_ids[:, k, :],
                                                 rownum[:, c:c + 1], None, ALU.is_equal)
                op.then_inc(onehot_ready, 1)

            def place_dense(i):
                dve.wait_ge(dense_loaded, 16 * (i + 1))
                wait(dve, gram_done, 4 * i)
                for h in range(2):
                    src = dense[:, :].rearrange("d (j h t) -> d j h t", h=2, t=QROWS)[:, :, h, :]
                    dst = emb[h][:, 0:EW].rearrange("d (j t f) -> d j t f", t=QROWS, f=FEATURES)
                    nc.vector.tensor_copy(dst[:, :, :, 0], src).then_inc(dense_placed, 1)

            def split_x(m, c):
                k = (c + 1) % XCHUNKS
                if k == 0:
                    wait(dve, l1_done, K1 * m)
                r, n = (128, 1) if c == PAIR_CHUNKS else (PAIR_ROWS, QUADS)
                dve.wait_ge(x_loaded[c], 16 * n * (m + 1))
                nc.vector.tensor_copy(xr[0][0:r, c, :], x[0:r, c, :]).then_inc(x_hi, 1)
                dve.wait_ge(x_hi, XCHUNKS * m + k + 1)
                nc.vector.tensor_tensor(xr[1][0:r, c, :], x[0:r, c, :],
                                        xr[0][0:r, c, :].bitcast(f32), ALU.subtract
                                        ).then_inc(x_split, 1)

            def split_h1(m):
                wait(dve, l2_done, K2 * m)
                for n in range(K1):
                    dve.wait_ge(h1_ready, K1 * m + n + 1)
                    nc.vector.tensor_copy(h1r[0][:, n, :], h1[:, n, :]).then_inc(h1_hi, 1)
                    dve.wait_ge(h1_hi, K1 * m + n + 1)
                    nc.vector.tensor_tensor(h1r[1][:, n, :], h1[:, n, :],
                                            h1r[0][:, n, :].bitcast(f32), ALU.subtract
                                            ).then_inc(h1_split, 1)

            def copy_y(m):
                dve.wait_ge(l3_done, m + 1)
                dve.sem_inc(dve_step, 1)
                nc.vector.tensor_copy(ycol[:, bass.ds(2 * m, 2)], ps_m[1][:, 0:2]
                                      ).then_inc(y_copied, 1)

            dve.wait_ge(consts_loaded, 16 * 5)
            for h in range(2):
                nc.vector.memset(emb[h][:, EW:], 0.0)
            for k in range(NO):
                split_lo(k)
                make_onehot(0, k)
            place_dense(0)
            for n in range(NO, len(items)):
                split_lo(n)
            for k in range(2):
                make_onehot(1, k)

            def body(i, last=False):
                for k in range(2, 5):
                    make_onehot(i, k)
                place_dense(i)
                split_x(i - 1, PAIR_CHUNKS)
                for k in range(5, NO):
                    make_onehot(i, k)
                for c in range(PAIR_CHUNKS):
                    split_x(i - 1, c)
                split_h1(i - 1)
                if not last:
                    for k in range(2):
                        make_onehot(i + 1, k)
                copy_y(i - 1)

            with dve.Fori(1, BLOCKS - 1) as i:
                body(i)
            body(BLOCKS - 1, last=True)
            for c in (PAIR_CHUNKS, *range(PAIR_CHUNKS)):
                split_x(BLOCKS - 1, c)
            split_h1(BLOCKS - 1)
            copy_y(BLOCKS - 1)
            dve.wait_ge(y_turned, 1)
            nc.vector.tensor_copy(yrow[:, :], ps_t[0][0:2 * BLOCKS, 0:128]).then_inc(y_row, 1)


def kernel(**inputs):
    import concourse.bacc as bacc
    from concourse.bass_utils import run_bass_kernel_spmd

    a = {k: np.asarray(v) for k, v in inputs.items()}
    ids = a["ids"].reshape(BLOCKS, 4, 2, 32, FIELDS)
    gather_ids = ids[..., GATHER].transpose(0, 2, 1, 3, 4).reshape(2 * BLOCKS, HALF, len(GATHER))
    onehot_ids = a["ids"].reshape(BLOCKS, BLOCK, FIELDS)[..., ONEHOT].transpose(0, 2, 1)
    dense_t = a["r_dense_features"].reshape(BLOCKS, BLOCK, DIM).transpose(0, 2, 1)
    w1 = a["W_top1"]
    row_of, n = {}, DIM
    for f in range(FEATURES):
        for g in range(f + 1, FEATURES):
            row_of[f, g] = n
            n += 1
    order = [row_of[tuple(sorted((SLOTS[f], SLOTS[(f + k) % FEATURES])))]
             for f in range(FEATURES) for k in range(1, SHIFTS + 1)]
    w1_pairs = w1[order].reshape(PAIR_CHUNKS, PAIR_ROWS, N1).transpose(1, 0, 2)
    w1_dense = np.stack([w1[:DIM], w1[n:]], axis=1)
    named = {
        "dense_t": dense_t,
        "gather_ids": gather_ids,
        "onehot_ids": onehot_ids.reshape(BLOCKS, 1, len(ONEHOT) * BLOCK),
        "tables": [a[f"tbl_{f}"] for f in GATHER],
        "small_tables": [a[f"tbl_{f}"] for f in ONEHOT],
        "row_numbers": np.arange(SMALL_ROWS, dtype=np.float32).reshape(SMALL_ROWS // 8, 8),
        "identity": np.eye(128, dtype=np.float32),
        "w1_pairs": w1_pairs,
        "w1_dense": w1_dense,
        "b1": a["b_top1"].reshape(N1 // 128, 128).T,
        "w2": a["W_top2"].reshape(N1 // 128, 128, N2).transpose(1, 0, 2),
        "b2": a["b_top2"].reshape(N2 // 128, 128).T,
        "w3": a["W_top3"].reshape(N2 // 128, 128).T,
    }
    nc = bacc.Bacc("TRN2", target_bir_lowering=False, num_devices=1)
    arrays = {}

    def declare(name, array):
        array = np.ascontiguousarray(array)
        arrays[name] = array
        return nc.dram_tensor(name, array.shape, mybir.dt.from_np(array.dtype), kind="ExternalInput").ap()

    args = {}
    for name, v in named.items():
        args[name] = ([declare(f"{name}_{n}", t) for n, t in enumerate(v)] if isinstance(v, list)
                      else declare(name, v))
    args["out"] = nc.dram_tensor("out", (2 * BLOCKS, HALF), mybir.dt.float32, kind="ExternalOutput").ap()
    build_tower(nc, **args)
    result = run_bass_kernel_spmd(nc, [arrays], core_ids=[0])
    return result.results[0]["out"].reshape(BATCH, 1)
```

```python
from contextlib import ExitStack

import concourse.bass as bass
import numpy as np
from concourse import mybir

BATCH, FIELDS, DIM = 2048, 26, 128
FEATURES = FIELDS + 1
SMALL_ROWS = 1000
ONEHOT = [3, 7, 9, 10, 11, 13, 15, 17]
GATHER = [f for f in range(FIELDS) if f not in ONEHOT]
SLOTS = [0] + [1 + f for f in GATHER] + [1 + f for f in ONEHOT]
HALF = 128
BLOCK = 2 * HALF
BLOCKS = BATCH // BLOCK
SHIFTS = FEATURES // 2
PAIR_F = 9
PAIR_CHUNKS = FEATURES // PAIR_F
PAIR_ROWS = PAIR_F * SHIFTS
N1, N2 = 512, 256


def build_tower(nc, dense_t, gather_ids, onehot_ids, tables, small_tables, row_numbers,
                identity, w1_pairs, w1_dense, b1, w2, b2, w3, out):
    f32, f32r, i32 = mybir.dt.float32, mybir.dt.float32r, mybir.dt.int32
    ALU, ACT = mybir.AluOpType, mybir.ActivationFunctionType

    NG, NO = len(GATHER), len(ONEHOT)
    GROUP = 4
    GROUPS = [(s, min(GROUP, NG - s)) for s in range(0, NG, GROUP)]
    NGR = len(GROUPS)
    TCHUNKS = 8
    TPART = SMALL_ROWS // TCHUNKS
    UNITS = [range(k, min(k + 2, NO)) for k in range(0, NO, 2)]
    NU = len(UNITS)
    QUADS, QROWS = 4, 32
    BANK_ROWS = QROWS // 2
    WRAP = FEATURES + SHIFTS
    BANDS = [(f, min(f + SHIFTS + 1, FEATURES)) for f in (0, SHIFTS + 1)]
    TB = BLOCK // QUADS
    XCHUNKS = PAIR_CHUNKS + 1
    K1, K2 = N1 // 128, N2 // 128

    scratch = nc.dram_tensor("interaction_scratch", (FEATURES, WRAP, QUADS, TB), f32,
                             kind="Internal").ap()

    ctx = ExitStack()
    with ctx:
        def sb(name, shape, dt=f32):
            return ctx.enter_context(nc.sbuf_tensor(name, shape, dt))

        def sem(name):
            return ctx.enter_context(nc.semaphore(name))

        ident = sb("ident", [128, 128])
        rownum = sb("rownum", [TPART, TCHUNKS])
        idx = [sb(f"idx{h}", [128, NG], i32) for h in range(2)]
        oh_ids = sb("oh_ids", [TPART, NO, BLOCK], i32)
        rows = [sb(f"rows{h}", [128, NG, DIM]) for h in range(2)]
        EW = HALF * FEATURES
        emb = [sb(f"emb{h}", [128, EW + 32 - FEATURES]) for h in range(2)]
        tbl = [sb(f"tbl_{p}", [TPART, NO, TCHUNKS, DIM], f32r) for p in ("hi", "lo")]
        onehot = [sb(f"onehot{s}", [TPART, TCHUNKS, BLOCK], f32r) for s in range(2)]
        dense = sb("dense", [128, BLOCK])
        inter = sb("inter", [128, WRAP, TB])
        x = sb("x", [128, XCHUNKS, BLOCK])
        xr = [sb(f"x_{p}", [128, XCHUNKS, BLOCK], f32r) for p in ("hi", "lo")]
        w1r = [sb(f"w1_{p}", [128, XCHUNKS, N1], f32r) for p in ("hi", "lo")]
        w2r = [sb(f"w2_{p}", [128, K1, N2], f32r) for p in ("hi", "lo")]
        w3s = sb("w3s", [128, K2])
        b1s = sb("b1s", [128, K1])
        b2s = sb("b2s", [128, K2])
        h1 = sb("h1", [128, K1, BLOCK])
        h1r = [sb(f"h1_{p}", [128, K1, BLOCK], f32r) for p in ("hi", "lo")]
        h2 = sb("h2", [128, K2, BLOCK])
        stage = [t[:, :, :].rearrange("p c b -> p (c b)") for t in (x, h1)]
        ycol = sb("ycol", [128, 2 * BLOCKS])
        yrow = sb("yrow", [2 * BLOCKS, 128])

        def pb(name):
            return ctx.enter_context(nc.psum_tensor(name, [128, 512], f32))

        ps_t = [pb(f"ps_t{b}") for b in range(2)]
        ps_o = [pb(f"ps_o{b}") for b in range(2)]
        ps_g = [pb(f"ps_g{b}") for b in range(2)]
        ps_m = [pb(f"ps_m{b}") for b in range(2)]

        last_l1 = [p[:, 0:BLOCK] for p in (*ps_o, *ps_t)]
        last_l2 = [p[:, 0:BLOCK] for p in ps_g]

        rownum_loaded = sem("rownum_loaded")
        ident_loaded = sem("ident_loaded")
        w3_biases_loaded = sem("w3_biases_loaded")
        stage_loaded = [sem(f"stage_loaded{s}") for s in range(2)]
        idx_loaded = [sem(f"idx_loaded{h}") for h in range(2)]
        oh_ids_loaded = sem("oh_ids_loaded")
        dense_loaded = sem("dense_loaded")
        gathered = [[sem(f"gathered{h}_{g}") for g in range(NGR)] for h in range(2)]
        stage_split = sem("stage_split")
        onehot_ready = sem("onehot_ready")
        onehot_used = sem("onehot_used")
        onehot_placed = sem("onehot_placed")
        dense_placed = sem("dense_placed")
        transposed = sem("transposed")
        rows_placed = sem("rows_placed")
        gram_done = sem("gram_done")
        gram_copied = sem("gram_copied")
        inter_stored = [sem(f"inter_stored{b}") for b in range(len(BANDS))]
        x_loaded = [sem(f"x_loaded{c}") for c in range(XCHUNKS)]
        stage_hi = sem("stage_hi")
        w1_dense_added = sem("w1_dense_added")
        x_hi = sem("x_hi")
        h1_hi = sem("h1_hi")
        x_split = sem("x_split")
        l1_done = sem("l1_done")
        h1_ready = sem("h1_ready")
        h1_split = sem("h1_split")
        l2_done = sem("l2_done")
        h2_ready = sem("h2_ready")
        l3_done = sem("l3_done")
        y_copied = sem("y_copied")
        y_turned = sem("y_turned")
        y_row = sem("y_row")
        pool_step, sp_step, dve_step = sem("pool_step"), sem("sp_step"), sem("dve_step")
        out_stored = sem("out_stored")

        def wait(eng, s, value):
            if not isinstance(value, int) or value > 0:
                eng.wait_ge(s, value)

        items = [(small_tables[k].rearrange("(p c) d -> p (c d)", c=TCHUNKS), TPART, TCHUNKS * DIM)
                 for k in range(NO)]
        items += [(w1_pairs[:, 0:2, :].rearrange("p c n -> p (c n)"), PAIR_ROWS, 2 * N1),
                  (w1_pairs[:, 2, :], PAIR_ROWS, N1),
                  (w1_dense.rearrange("p c n -> p (c n)"), 128, 2 * N1),
                  (w2.rearrange("p c n -> p (c n)"), 128, K1 * N2)]

        DENSE_ITEM = NO + 2

        def split_of(n):
            if n < NO:
                parts = [t[:, n, :, :].rearrange("p c d -> p (c d)") for t in tbl]
            elif n == NO:
                parts = [t[0:PAIR_ROWS, 0:2, :].rearrange("p c n -> p (c n)") for t in w1r]
            elif n == NO + 1:
                parts = [t[0:PAIR_ROWS, 2, :] for t in w1r]
            elif n == DENSE_ITEM:
                parts = [t[:, PAIR_CHUNKS, :] for t in w1r]
            else:
                parts = [t[:, :, :].rearrange("p c n -> p (c n)") for t in w2r]
            return (N1 if n in (NO + 1, DENSE_ITEM) else 1024, *parts)

        block = ctx.enter_context(nc.Block())

        @block.sync
        def _(sp):
            def load_idx(i, h):
                sp.dma_start(idx[h][:, :], gather_ids[2 * i + h]).then_inc(idx_loaded[h], 16)

            def load_oh_ids(i):
                src = onehot_ids[i]
                sp.dma_start(oh_ids[:, :, :].rearrange("p k b -> p (k b)"),
                             src.to_broadcast([TPART, NO * BLOCK])).then_inc(oh_ids_loaded, 16)

            def load_dense(i):
                sp.dma_start(dense[:, :], dense_t[i]).then_inc(dense_loaded, 16)

            def load_stage(n):
                src, r, w = items[n]
                if n >= 2:
                    sp.wait_ge(stage_split, n - 1)
                sp.dma_start(stage[n % 2][0:r, 0:w], src).then_inc(stage_loaded[n % 2], 16)

            def next_idx(i, h):
                sp.wait_ge(transposed, NGR * (2 * i + h + 1))
                sp.sem_inc(sp_step, 1)
                load_idx(i + 1, h)

            def next_dense(i):
                sp.wait_ge(dense_placed, 2 * (i + 1))
                sp.sem_inc(sp_step, 1)
                load_dense(i + 1)

            def next_oh_ids(i):
                sp.wait_ge(onehot_ready, NO * (i + 1))
                sp.sem_inc(sp_step, 1)
                load_oh_ids(i + 1)

            def next_block_loads(i):
                next_dense(i)
                next_idx(i, 0)
                next_oh_ids(i)
                next_idx(i, 1)

            def turn_interactions(i):
                wait(sp, x_split, XCHUNKS * i)
                sp.sem_inc(sp_step, 1)
                sp.dma_start(x[:, PAIR_CHUNKS, :], dense_t[i]).then_inc(x_loaded[PAIR_CHUNKS], 16)
                sp.wait_ge(gram_copied, 8 * (i + 1))
                sp.sem_inc(sp_step, 1)
                for b, (f0, f1) in enumerate(BANDS):
                    for j in range(QUADS):
                        g0, g1 = f0 + 1, f1 + SHIFTS
                        sp.dma_start(scratch[f0:f1, g0:g1, j, :],
                                     inter[QROWS * j + f0:QROWS * j + f1, g0:g1, :]
                                     ).then_inc(inter_stored[b], 16)
                for c in range(PAIR_CHUNKS):
                    b = (PAIR_F * (c + 1) - 1) // BANDS[0][1]
                    sp.wait_ge(inter_stored[b], 16 * QUADS * (i + 1))
                    src = bass.AP(tensor=scratch.tensor,
                                  offset=(PAIR_F * c * (WRAP + 1) + 1) * BLOCK,
                                  ap=[[(WRAP + 1) * BLOCK, PAIR_F], [BLOCK, SHIFTS], [1, BLOCK]])
                    sp.dma_start(x[0:PAIR_ROWS, c, :], src).then_inc(x_loaded[c], 16)

            load_idx(0, 0)
            load_stage(0)
            sp.dma_start(rownum[:, :], row_numbers).then_inc(rownum_loaded, 16)
            load_oh_ids(0)
            load_stage(1)
            sp.dma_start(ident[:, :], identity).then_inc(ident_loaded, 16)
            load_dense(0)
            load_idx(0, 1)
            for dst, src in ((w3s, w3), (b1s, b1), (b2s, b2)):
                sp.dma_start(dst[:, :], src).then_inc(w3_biases_loaded, 16)
            for n in range(2, len(items)):
                if n == NO:
                    next_dense(0)
                    next_idx(0, 0)
                if n == NO + 1:
                    next_oh_ids(0)
                load_stage(n)
            next_idx(0, 1)
            sp.wait_ge(stage_split, len(items))
            turn_interactions(0)
            with sp.Fori(1, BLOCKS - 1) as i:
                next_block_loads(i)
                turn_interactions(i)
            turn_interactions(BLOCKS - 1)
            sp.wait_ge(y_row, 1)
            sp.dma_start(out, yrow[:, :]).then_inc(out_stored, 16)
            sp.wait_ge(out_stored, 16)

        @block.gpsimd
        def _(pool):
            def gather_half(i, h):
                pool.wait_ge(idx_loaded[h], 16 * (i + 1))
                for g, (s, n) in enumerate(GROUPS):
                    wait(pool, transposed, 2 * NGR * (i - 1) + NGR * h + g + 1)
                    pool.sem_inc(pool_step, 1)
                    for k in range(s, s + n):
                        pool.indirect_dma_start(
                            rows[h][:, k, :], None, tables[k],
                            bass.IndirectOffsetOnAxis(ap=idx[h][:, k:k + 1], axis=0),
                        ).then_inc(gathered[h][g], 16)

            gather_half(0, 0)
            gather_half(0, 1)
            with pool.Fori(1, BLOCKS) as i:
                gather_half(i, 0)
                gather_half(i, 1)

        @block.tensor
        def _(pe):
            def onehot_lookups(i, fields):
                for k in fields:
                    u = k // 2
                    if isinstance(i, int) and i == 0:
                        pe.wait_ge(stage_split, k + 1)
                    pe.wait_ge(onehot_ready, NO * i + k + 1)
                    if k % 2 == 0:
                        wait(pe, onehot_placed, 2 * (NU * i + (u - 1 if u else 0)))
                    o = ps_o[u % 2][:, BLOCK * (k % 2):BLOCK * (k % 2 + 1)]
                    for c in range(TCHUNKS):
                        for p in range(2):
                            mm = pe.matmul(o, tbl[p][:, k, c, :], onehot[k % 2][:, c, :],
                                           start=(c + p == 0), stop=(c == TCHUNKS - 1 and p == 1))
                    mm.then_inc(onehot_used, 1)

            def transposes(i, h, g):
                s, n = GROUPS[g]
                q = NGR * h + g
                pe.wait_ge(gathered[h][g], 16 * n * (i + 1))
                wait(pe, rows_placed, 2 * NGR * i + q - 1)
                for k in range(n):
                    mm = pe.transpose(ps_t[q % 2][:, 128 * k:128 * (k + 1)], rows[h][:, s + k, :],
                                      ident[:, :])
                mm.then_inc(transposed, 1)

            def grams(i, h, q):
                if q == 0:
                    pe.wait_ge(rows_placed, 2 * NGR * i + NGR * (h + 1))
                    pe.wait_ge(onehot_placed, 2 * NU * (i + 1))
                    pe.wait_ge(dense_placed, 2 * (i + 1))
                wait(pe, gram_copied, 2 * (4 * i + 2 * h + q - 1))
                for u in range(BANK_ROWS):
                    for j in range(QUADS):
                        a = (QROWS * j + BANK_ROWS * q + u) * FEATURES
                        mm = pe.matmul(
                            ps_g[q][QROWS * j:QROWS * (j + 1), FEATURES * u:FEATURES * (u + 1)],
                            emb[h][:, a:a + QROWS], emb[h][:, a:a + FEATURES],
                            start=True, stop=True, tile_position=(0, QROWS * j))
                mm.then_inc(gram_done, 1)

            def split_products(o, w, v, chunks, n, ready=None):
                terms = [(c, a, b) for c in chunks for a, b in ((0, 0), (0, 1), (1, 0))]
                for m, (c, a, b) in enumerate(terms):
                    if ready and (a, b) == (0, 0):
                        pe.wait_ge(*ready(c))
                    r = PAIR_ROWS if w is w1r and c < PAIR_CHUNKS else 128
                    mm = pe.matmul(o, w[a][0:r, c, 128 * n:128 * (n + 1)], v[b][0:r, c, :],
                                   start=(m == 0), stop=(m == len(terms) - 1))
                return mm

            def layer1(m, n):
                if n == 0:
                    pe.wait_ge(stage_split, len(items))
                    wait(pe, h2_ready, K2 * m)
                if n == 2:
                    wait(pe, y_copied, m)
                o = ps_m[n // 2][:, BLOCK * (n % 2):BLOCK * (n % 2 + 1)]
                order = (PAIR_CHUNKS, *range(PAIR_CHUNKS))
                split_products(o, w1r, xr, order, n,
                               (lambda c: (x_split, XCHUNKS * m + order.index(c) + 1)) if n == 0 else None
                               ).then_inc(l1_done, 1)

            def layer2(m, n):
                if n == 0:
                    pe.wait_ge(h1_split, K1 * (m + 1))
                o = ps_m[0][:, BLOCK * n:BLOCK * (n + 1)]
                split_products(o, w2r, h1r, range(K1), n).then_inc(l2_done, 1)

            def layer3(m):
                pe.wait_ge(h2_ready, K2 * (m + 1))
                for t in range(2):
                    for c in range(K2):
                        mm = pe.matmul(ps_m[1][:, t:t + 1], h2[:, c, 128 * t:128 * (t + 1)],
                                       w3s[:, c:c + 1], start=(c == 0), stop=(c == K2 - 1))
                mm.then_inc(l3_done, 1)

            def last_layer1(m, chunks):
                order = (PAIR_CHUNKS, *range(PAIR_CHUNKS))
                for c in chunks:
                    k = order.index(c)
                    if k == 0:
                        pe.wait_ge(rows_placed, 2 * NGR * (m + 1))
                        pe.wait_ge(onehot_placed, 2 * NU * (m + 1))
                    pe.wait_ge(x_split, XCHUNKS * m + k + 1)
                    r = PAIR_ROWS if c < PAIR_CHUNKS else 128
                    for n in range(K1):
                        for a, b in ((0, 0), (0, 1), (1, 0)):
                            mm = pe.matmul(last_l1[n], w1r[a][0:r, c, 128 * n:128 * (n + 1)],
                                           xr[b][0:r, c, :], start=(k + a + b == 0),
                                           stop=(k == XCHUNKS - 1 and a == 1))
                        if k == XCHUNKS - 1:
                            mm.then_inc(l1_done, 1)

            def last_layer2(m):
                pe.wait_ge(gram_copied, 8 * (m + 1))
                for c in range(K1):
                    pe.wait_ge(h1_split, K1 * m + c + 1)
                    for n in range(K2):
                        for a, b in ((0, 0), (0, 1), (1, 0)):
                            mm = pe.matmul(last_l2[n], w2r[a][:, c, 128 * n:128 * (n + 1)],
                                           h1r[b][:, c, :], start=(c + a + b == 0),
                                           stop=(c == K1 - 1 and a == 1))
                        if c == K1 - 1:
                            mm.then_inc(l2_done, 1)

            def body(i, first=False, last=False):
                if first:
                    onehot_lookups(i, UNITS[0])
                for u in range(1, NU):
                    transposes(i, 0, u - 1)
                    onehot_lookups(i, UNITS[u])
                for g in range(NU - 1, NGR):
                    transposes(i, 0, g)
                if first:
                    grams(i, 0, 0)
                    transposes(i, 1, 0)
                    transposes(i, 1, 1)
                    grams(i, 0, 1)
                    transposes(i, 1, 2)
                    onehot_lookups(i + 1, UNITS[0][:1])
                    for g in range(3, NGR):
                        transposes(i, 1, g)
                    grams(i, 1, 0)
                    onehot_lookups(i + 1, UNITS[0][1:])
                    grams(i, 1, 1)
                    return
                layer1(i - 1, 0)
                grams(i, 0, 0)
                if last:
                    layer1(i - 1, 1)
                    transposes(i, 1, 0)
                    transposes(i, 1, 1)
                    grams(i, 0, 1)
                    for g in range(2, NGR - 1):
                        transposes(i, 1, g)
                    layer1(i - 1, 2)
                    transposes(i, 1, NGR - 1)
                    layer1(i - 1, 3)
                    grams(i, 1, 0)
                    grams(i, 1, 1)
                    last_layer1(i, [PAIR_CHUNKS])
                    layer2(i - 1, 0)
                    layer2(i - 1, 1)
                    last_layer1(i, range(PAIR_CHUNKS))
                    layer3(i - 1)
                    last_layer2(i)
                    return
                layer1(i - 1, 1)
                transposes(i, 1, 0)
                transposes(i, 1, 1)
                grams(i, 0, 1)
                layer1(i - 1, 2)
                transposes(i, 1, 2)
                layer1(i - 1, 3)
                for g in range(3, NGR):
                    transposes(i, 1, g)
                onehot_lookups(i + 1, UNITS[0][:1])
                grams(i, 1, 0)
                layer2(i - 1, 0)
                layer2(i - 1, 1)
                grams(i, 1, 1)
                onehot_lookups(i + 1, UNITS[0][1:])
                layer3(i - 1)

            pe.wait_ge(ident_loaded, 16)
            body(0, first=True)
            pe.wait_ge(w3_biases_loaded, 16 * 3)
            with pe.Fori(1, BLOCKS - 1) as i:
                body(i)
            body(BLOCKS - 1, last=True)
            pe.wait_ge(y_copied, BLOCKS - 1)
            layer3(BLOCKS - 1)
            pe.wait_ge(y_copied, BLOCKS)
            pe.transpose(ps_t[0][0:2 * BLOCKS, 0:128], ycol[:, :], ident[:, :]).then_inc(y_turned, 1)

        @block.scalar
        def _(act):
            def split_hi(n):
                w, hi, lo = split_of(n)
                act.wait_ge(stage_loaded[n % 2], 16 * (n // 2 + 1))
                nc.scalar.activation(hi, stage[n % 2][0:items[n][1], 0:w], ACT.Copy
                                     ).then_inc(stage_hi, 1)

            def emb_view(h):
                return emb[h][:, 0:EW].rearrange("d (r f) -> d r f", f=FEATURES)

            def place_onehot(i, u):
                if u == 0:
                    wait(act, gram_done, 4 * i)
                n = len(UNITS[u])
                act.wait_ge(onehot_used, NO * i + 2 * u + n)
                f = 1 + NG + 2 * u
                for h in range(2):
                    src = ps_o[u % 2][:, 0:BLOCK * n].rearrange(
                        "d (k j h t) -> d k j h t", k=n, h=2, t=QROWS)[:, :, :, h, :]
                    dst = emb_view(h)[:, :, f:f + n].rearrange("d (j t) k -> d k j t", t=QROWS)
                    nc.scalar.activation(dst, src, ACT.Copy).then_inc(onehot_placed, 1)

            def place_rows(i, h, g):
                if g == 0:
                    wait(act, gram_done, 4 * (i - 1) + 2 * (h + 1))
                s, n = GROUPS[g]
                q = NGR * h + g
                act.wait_ge(transposed, 2 * NGR * i + q + 1)
                src = ps_t[q % 2][:, 0:128 * n].rearrange("d (k r) -> d r k", r=128)
                nc.scalar.activation(emb_view(h)[:, :, 1 + s:1 + s + n], src, ACT.Copy
                                     ).then_inc(rows_placed, 1)

            def copy_grams(i, h, q):
                if h == 0 and q == 0:
                    for s in inter_stored:
                        wait(act, s, 16 * QUADS * i)
                act.wait_ge(gram_done, 4 * i + 2 * h + q + 1)
                src = ps_g[q][:, 0:BANK_ROWS * FEATURES].rearrange("p (t g) -> p g t", g=FEATURES)
                t = QROWS * h + BANK_ROWS * q
                nc.scalar.activation(inter[:, 0:FEATURES, t:t + BANK_ROWS], src, ACT.Copy
                                     ).then_inc(gram_copied, 1)
                nc.scalar.activation(inter[:, FEATURES:WRAP, t:t + BANK_ROWS], src[:, 0:SHIFTS, :],
                                     ACT.Copy).then_inc(gram_copied, 1)

            def relu1(m, bank):
                if bank == 0:
                    wait(act, h1_split, K1 * m)
                act.wait_ge(l1_done, K1 * m + 2 * bank + 2)
                for n in (2 * bank, 2 * bank + 1):
                    nc.scalar.activation(h1[:, n, :], ps_m[bank][:, BLOCK * (n % 2):BLOCK * (n % 2 + 1)],
                                         ACT.Relu, bias=b1s[:, n:n + 1]).then_inc(h1_ready, 1)

            def relu2(m):
                wait(act, l3_done, m)
                act.wait_ge(l2_done, K2 * (m + 1))
                for n in range(K2):
                    nc.scalar.activation(h2[:, n, :], ps_m[0][:, BLOCK * n:BLOCK * (n + 1)],
                                         ACT.Relu, bias=b2s[:, n:n + 1]).then_inc(h2_ready, 1)

            def body(i, first=False, last=False):
                if first:
                    for k in (*UNITS[0], *UNITS[1]):
                        split_hi(k)
                place_onehot(i, 0)
                for u in range(1, NU):
                    place_rows(i, 0, u - 1)
                    if first and u + 1 < NU:
                        for k in UNITS[u + 1]:
                            split_hi(k)
                    place_onehot(i, u)
                for g in range(NU - 1, NGR):
                    place_rows(i, 0, g)
                if first:
                    copy_grams(i, 0, 0)
                    place_rows(i, 1, 0)
                    place_rows(i, 1, 1)
                    copy_grams(i, 0, 1)
                    for g in range(2, NGR):
                        place_rows(i, 1, g)
                    copy_grams(i, 1, 0)
                    copy_grams(i, 1, 1)
                    return
                copy_grams(i, 0, 0)
                if last:
                    place_rows(i, 1, 0)
                    place_rows(i, 1, 1)
                    copy_grams(i, 0, 1)
                    for g in range(2, NGR):
                        place_rows(i, 1, g)
                    relu1(i - 1, 0)
                    copy_grams(i, 1, 0)
                    copy_grams(i, 1, 1)
                    relu1(i - 1, 1)
                    relu2(i - 1)
                    return
                relu1(i - 1, 0)
                place_rows(i, 1, 0)
                place_rows(i, 1, 1)
                copy_grams(i, 0, 1)
                place_rows(i, 1, 2)
                relu1(i - 1, 1)
                for g in range(3, NGR):
                    place_rows(i, 1, g)
                copy_grams(i, 1, 0)
                relu2(i - 1)
                copy_grams(i, 1, 1)

            def last_relus(m):
                act.wait_ge(h1_split, K1 * m)
                for n in range(K1):
                    act.wait_ge(l1_done, K1 * m + n + 1)
                    nc.scalar.activation(h1[:, n, :], last_l1[n], ACT.Relu, bias=b1s[:, n:n + 1]
                                         ).then_inc(h1_ready, 1)
                act.wait_ge(l3_done, m)
                for n in range(K2):
                    act.wait_ge(l2_done, K2 * m + n + 1)
                    nc.scalar.activation(h2[:, n, :], last_l2[n], ACT.Relu, bias=b2s[:, n:n + 1]
                                         ).then_inc(h2_ready, 1)

            body(0, first=True)
            act.wait_ge(w3_biases_loaded, 16 * 3)
            with act.Fori(1, BLOCKS - 1) as i:
                body(i)
            body(BLOCKS - 1, last=True)
            last_relus(BLOCKS - 1)

        @block.vector
        def _(dve):
            def split_lo(n):
                r = items[n][1]
                w, hi, lo = split_of(n)
                s = stage[n % 2]
                if n == DENSE_ITEM:
                    dve.wait_ge(stage_loaded[n % 2], 16 * (n // 2 + 1))
                    nc.vector.tensor_tensor(s[:, 0:N1], s[:, 0:N1], s[:, N1:2 * N1], ALU.add
                                            ).then_inc(w1_dense_added, 1)
                    dve.wait_ge(w1_dense_added, 1)
                if n >= NO:
                    dve.wait_ge(stage_loaded[n % 2], 16 * (n // 2 + 1))
                    nc.vector.tensor_copy(hi, s[0:r, 0:w]).then_inc(stage_hi, 1)
                dve.wait_ge(stage_hi, n + 1)
                nc.vector.tensor_tensor(lo, s[0:r, 0:w], hi.bitcast(f32), ALU.subtract
                                        ).then_inc(stage_split, 1)

            def make_onehot(i, k):
                if k == 0:
                    dve.wait_ge(oh_ids_loaded, 16 * (i + 1))
                wait(dve, onehot_used, NO * i + (k - 1 if k else 0))
                for c in range(TCHUNKS):
                    op = nc.vector.tensor_scalar(onehot[k % 2][:, c, :], oh_ids[:, k, :],
                                                 rownum[:, c:c + 1], None, ALU.is_equal)
                op.then_inc(onehot_ready, 1)

            def place_dense(i):
                dve.wait_ge(dense_loaded, 16 * (i + 1))
                wait(dve, gram_done, 4 * i)
                for h in range(2):
                    src = dense[:, :].rearrange("d (j h t) -> d j h t", h=2, t=QROWS)[:, :, h, :]
                    dst = emb[h][:, 0:EW].rearrange("d (j t f) -> d j t f", t=QROWS, f=FEATURES)
                    nc.vector.tensor_copy(dst[:, :, :, 0], src).then_inc(dense_placed, 1)

            def split_x(m, c):
                k = (c + 1) % XCHUNKS
                if k == 0:
                    wait(dve, l1_done, K1 * m)
                r = 128 if c == PAIR_CHUNKS else PAIR_ROWS
                dve.wait_ge(x_loaded[c], 16 * (m + 1))
                nc.vector.tensor_copy(xr[0][0:r, c, :], x[0:r, c, :]).then_inc(x_hi, 1)
                dve.wait_ge(x_hi, XCHUNKS * m + k + 1)
                nc.vector.tensor_tensor(xr[1][0:r, c, :], x[0:r, c, :],
                                        xr[0][0:r, c, :].bitcast(f32), ALU.subtract
                                        ).then_inc(x_split, 1)

            def split_h1(m, chunks=range(K1)):
                if 0 in chunks:
                    wait(dve, l2_done, K2 * m)
                for n in chunks:
                    dve.wait_ge(h1_ready, K1 * m + n + 1)
                    nc.vector.tensor_copy(h1r[0][:, n, :], h1[:, n, :]).then_inc(h1_hi, 1)
                    dve.wait_ge(h1_hi, K1 * m + n + 1)
                    nc.vector.tensor_tensor(h1r[1][:, n, :], h1[:, n, :],
                                            h1r[0][:, n, :].bitcast(f32), ALU.subtract
                                            ).then_inc(h1_split, 1)

            def copy_y(m):
                dve.wait_ge(l3_done, m + 1)
                dve.sem_inc(dve_step, 1)
                nc.vector.tensor_copy(ycol[:, bass.ds(2 * m, 2)], ps_m[1][:, 0:2]
                                      ).then_inc(y_copied, 1)

            for h in range(2):
                nc.vector.memset(emb[h][:, EW:], 0.0)
            for k in range(NO):
                split_lo(k)
                if k == 0:
                    dve.wait_ge(rownum_loaded, 16)
                make_onehot(0, k)
                if k == 1:
                    place_dense(0)
            split_lo(NO)
            for k in range(3):
                make_onehot(1, k)
            for n in range(NO + 1, len(items)):
                split_lo(n)
                if n == NO + 1:
                    make_onehot(1, 3)

            def body(i, last=False):
                make_onehot(i, 4)
                place_dense(i)
                for k in range(5, NO):
                    make_onehot(i, k)
                for c in (PAIR_CHUNKS, *range(PAIR_CHUNKS)):
                    split_x(i - 1, c)
                if not last:
                    make_onehot(i + 1, 0)
                if last:
                    split_h1(i - 1, [0, 1])
                    split_x(i, PAIR_CHUNKS)
                    split_h1(i - 1, [2, 3])
                else:
                    split_h1(i - 1)
                    make_onehot(i + 1, 1)
                    make_onehot(i + 1, 2)
                    make_onehot(i + 1, 3)
                    copy_y(i - 1)

            with dve.Fori(1, BLOCKS - 1) as i:
                body(i)
            body(BLOCKS - 1, last=True)
            for c in range(PAIR_CHUNKS):
                split_x(BLOCKS - 1, c)
            split_h1(BLOCKS - 1)
            copy_y(BLOCKS - 2)
            copy_y(BLOCKS - 1)
            dve.wait_ge(y_turned, 1)
            nc.vector.tensor_copy(yrow[:, :], ps_t[0][0:2 * BLOCKS, 0:128]).then_inc(y_row, 1)


def kernel(**inputs):
    import concourse.bacc as bacc
    from concourse.bass_utils import run_bass_kernel_spmd

    a = {k: np.asarray(v) for k, v in inputs.items()}
    ids = a["ids"].reshape(BLOCKS, 4, 2, 32, FIELDS)
    gather_ids = ids[..., GATHER].transpose(0, 2, 1, 3, 4).reshape(2 * BLOCKS, HALF, len(GATHER))
    onehot_ids = a["ids"].reshape(BLOCKS, BLOCK, FIELDS)[..., ONEHOT].transpose(0, 2, 1)
    dense_t = a["r_dense_features"].reshape(BLOCKS, BLOCK, DIM).transpose(0, 2, 1)
    w1 = a["W_top1"]
    row_of, n = {}, DIM
    for f in range(FEATURES):
        for g in range(f + 1, FEATURES):
            row_of[f, g] = n
            n += 1
    order = [row_of[tuple(sorted((SLOTS[f], SLOTS[(f + k) % FEATURES])))]
             for f in range(FEATURES) for k in range(1, SHIFTS + 1)]
    w1_pairs = w1[order].reshape(PAIR_CHUNKS, PAIR_ROWS, N1).transpose(1, 0, 2)
    w1_dense = np.stack([w1[:DIM], w1[n:]], axis=1)
    named = {
        "dense_t": dense_t,
        "gather_ids": gather_ids,
        "onehot_ids": onehot_ids.reshape(BLOCKS, 1, len(ONEHOT) * BLOCK),
        "tables": [a[f"tbl_{f}"] for f in GATHER],
        "small_tables": [a[f"tbl_{f}"] for f in ONEHOT],
        "row_numbers": np.arange(SMALL_ROWS, dtype=np.float32).reshape(SMALL_ROWS // 8, 8),
        "identity": np.eye(128, dtype=np.float32),
        "w1_pairs": w1_pairs,
        "w1_dense": w1_dense,
        "b1": a["b_top1"].reshape(N1 // 128, 128).T,
        "w2": a["W_top2"].reshape(N1 // 128, 128, N2).transpose(1, 0, 2),
        "b2": a["b_top2"].reshape(N2 // 128, 128).T,
        "w3": a["W_top3"].reshape(N2 // 128, 128).T,
    }
    nc = bacc.Bacc("TRN2", target_bir_lowering=False, num_devices=1)
    arrays = {}

    def declare(name, array):
        array = np.ascontiguousarray(array)
        arrays[name] = array
        return nc.dram_tensor(name, array.shape, mybir.dt.from_np(array.dtype), kind="ExternalInput").ap()

    args = {}
    for name, v in named.items():
        args[name] = ([declare(f"{name}_{n}", t) for n, t in enumerate(v)] if isinstance(v, list)
                      else declare(name, v))
    args["out"] = nc.dram_tensor("out", (2 * BLOCKS, HALF), mybir.dt.float32, kind="ExternalOutput").ap()
    build_tower(nc, **args)
    result = run_bass_kernel_spmd(nc, [arrays], core_ids=[0])
    return result.results[0]["out"].reshape(BATCH, 1)
```
